# Optimizing a Trainium2 kernel written in Bass

```python
import numpy as np
import jax
import jax.numpy as jnp

def _softmax(x, axis=-1):
    return jax.nn.softmax(x, axis=axis)

def _gelu(x):
    return jax.nn.gelu(x, approximate=True)

def _silu(x):
    return jax.nn.silu(x)

def _sigmoid(x):
    return jax.nn.sigmoid(x)

def _layernorm(x, axis=-1, eps=1e-05):
    m = jnp.mean(x, axis=axis, keepdims=True)
    v = jnp.var(x, axis=axis, keepdims=True)
    return (x - m) / jnp.sqrt(v + eps)

def _scatter_add(tgt, idx, src, axis=0):
    return tgt.at[idx].add(src)

def _segment_sum(src, seg, n):
    return jax.ops.segment_sum(src, seg, n)
kernel_name = 'mk_gnn_preln_d1_gnn_r32_74690e'

def setup_inputs(seed: int=0):
    np.random.seed(seed)
    _w = jnp.asarray

    def _rec_inputs():
        import jax
        import jax.numpy as jnp
        _gk = jax.random.key(seed)
        x = -0.0005121 + 1.001 * jax.random.normal(jax.random.fold_in(_gk, 1), (50000, 160), jnp.float32)
        src = jax.random.randint(jax.random.fold_in(_gk, 2), (50000,), 0, 50000, jnp.int32)
        dst = jax.random.randint(jax.random.fold_in(_gk, 3), (50000,), 0, 50000, jnp.int32)
        _o = jnp.argsort(dst, stable=True)
        src = src[_o]
        dst = dst[_o]
        edge_attr_4 = 0.000735704 + 1.0001 * jax.random.normal(jax.random.fold_in(_gk, 11), (50000, 4), jnp.float32)
        node_vec1 = -0.00719938 + 0.999885 * jax.random.normal(jax.random.fold_in(_gk, 13), (50000, 1), jnp.float32)
        return (x, src, dst, edge_attr_4, node_vec1)
    x, src, dst, edge_attr_4, node_vec1 = _rec_inputs()

    def _L0_gnn_setup():
        import jax, jax.numpy as jnp
        import numpy as np
        N = 625
        E = 20000
        INV_SQRT3 = 0.5773502691896258
        INV8 = 0.125
        INV_SQRT32 = 0.17677669529663687
        INV64 = 0.015625
        INV32 = 0.03125
        INV_SQRT2048 = 0.022097086912079608
        key = jax.random.key(seed)
        ks = jax.random.split(key, 16)
        f32 = jnp.float32
        return {'node_features': jax.random.normal(ks[0], (N, 160), f32), 'edge_index': jax.random.randint(ks[1], (2, E), 0, N), 'edge_attr_tensor': jax.random.normal(ks[2], (E, 4), f32), 'node_attr_scalar_raw': jax.random.normal(ks[3], (N, 1), f32), 'Wm_ss': jax.random.normal(ks[4], (64, 64), f32), 'Wm_vv': jax.random.normal(ks[5], (32, 64), f32), 'Wm_sv': jax.random.normal(ks[6], (64, 32), f32), 'Wm_vs': jax.random.normal(ks[7], (32, 32), f32), 'Lm_s': jax.random.normal(ks[8], (64, 64), f32), 'Lm_v': jax.random.normal(ks[9], (32, 32), f32), 'Wu_ss': jax.random.normal(ks[10], (64, 64, 64), f32), 'Wu_vv': jax.random.normal(ks[11], (32, 32, 64), f32), 'Wu_sv': jax.random.normal(ks[12], (64, 32, 32), f32), 'Wu_vs': jax.random.normal(ks[13], (32, 64, 32), f32), 'Lu_s': jax.random.normal(ks[14], (64, 64), f32), 'Lu_v': jax.random.normal(ks[15], (32, 32), f32)}
    _L0_gnn_all = _L0_gnn_setup()
    _L0_gnn_in = {k: v for k, v in _L0_gnn_all.items() if k in ('Wm_ss', 'Wm_vv', 'Wm_sv', 'Wm_vs', 'Lm_s', 'Lm_v', 'Wu_ss', 'Wu_vv', 'Wu_sv', 'Wu_vs', 'Lu_s', 'Lu_v')}
    del _L0_gnn_all
    return {'x': x, 'src': src, 'dst': dst, 'edge_attr_4': edge_attr_4, 'node_vec1': node_vec1, 'L0_gnn_Wm_ss': _L0_gnn_in['Wm_ss'], 'L0_gnn_Wm_vv': _L0_gnn_in['Wm_vv'], 'L0_gnn_Wm_sv': _L0_gnn_in['Wm_sv'], 'L0_gnn_Wm_vs': _L0_gnn_in['Wm_vs'], 'L0_gnn_Lm_s': _L0_gnn_in['Lm_s'], 'L0_gnn_Lm_v': _L0_gnn_in['Lm_v'], 'L0_gnn_Wu_ss': _L0_gnn_in['Wu_ss'], 'L0_gnn_Wu_vv': _L0_gnn_in['Wu_vv'], 'L0_gnn_Wu_sv': _L0_gnn_in['Wu_sv'], 'L0_gnn_Wu_vs': _L0_gnn_in['Wu_vs'], 'L0_gnn_Lu_s': _L0_gnn_in['Lu_s'], 'L0_gnn_Lu_v': _L0_gnn_in['Lu_v']}

def reference(x, src, dst, edge_attr_4, node_vec1, L0_gnn_Wm_ss, L0_gnn_Wm_vv, L0_gnn_Wm_sv, L0_gnn_Wm_vs, L0_gnn_Lm_s, L0_gnn_Lm_v, L0_gnn_Wu_ss, L0_gnn_Wu_vv, L0_gnn_Wu_sv, L0_gnn_Wu_vs, L0_gnn_Lu_s, L0_gnn_Lu_v):
    import jax
    import jax.numpy as jnp

    def _L0_gnn_ref(node_features, edge_index, edge_attr_tensor, node_attr_scalar_raw, Wm_ss, Wm_vv, Wm_sv, Wm_vs, Lm_s, Lm_v, Wu_ss, Wu_vv, Wu_sv, Wu_vs, Lu_s, Lu_v):
        import jax, jax.numpy as jnp
        import numpy as np
        N = 625
        E = 20000
        INV_SQRT3 = 0.5773502691896258
        INV8 = 0.125
        INV_SQRT32 = 0.17677669529663687
        INV64 = 0.015625
        INV32 = 0.03125
        INV_SQRT2048 = 0.022097086912079608
        n = node_features.shape[0]
        e = edge_attr_tensor.shape[0]
        row, col = (edge_index[0], edge_index[1])
        r_vec = edge_attr_tensor[:, :3]
        dist = edge_attr_tensor[:, 3:4]
        xj = node_features[col]
        s = xj[:, :64]
        v = xj[:, 64:].reshape(e, 32, 3)
        m0 = s @ Wm_ss * dist * INV8 + jnp.einsum('eui,ei->eu', v, r_vec) @ Wm_vv * (INV_SQRT3 * INV_SQRT32)
        m1 = (s @ Wm_sv)[:, :, None] * r_vec[:, None, :] * INV8 + jnp.einsum('eui,uw->ewi', v, Wm_vs) * dist[:, :, None] * INV_SQRT32
        m0 = m0 + s @ Lm_s * INV8
        m1 = m1 + jnp.einsum('eui,uw->ewi', v, Lm_v) * INV_SQRT32
        msg = jnp.concatenate([m0, m1.reshape(e, 96)], axis=-1)
        agg = jax.ops.segment_sum(msg, row, num_segments=n)
        a0 = agg[:, :64]
        a1 = agg[:, 64:].reshape(n, 32, 3)
        xs = node_features[:, :64]
        xv = node_features[:, 64:].reshape(n, 32, 3)
        u0 = jnp.einsum('nu,nv,uvw->nw', xs, a0, Wu_ss) * INV64 + jnp.einsum('nui,nvi,uvw->nw', xv, a1, Wu_vv) * (INV_SQRT3 * INV32)
        u1 = jnp.einsum('nu,nvi,uvw->nwi', xs, a1, Wu_sv) * INV_SQRT2048 + jnp.einsum('nui,nv,uvw->nwi', xv, a0, Wu_vs) * INV_SQRT2048
        u0 = u0 + xs @ Lu_s * INV8
        u1 = u1 + jnp.einsum('nui,uw->nwi', xv, Lu_v) * INV_SQRT32
        upd = jnp.concatenate([u0, u1.reshape(n, 96)], axis=-1)
        return node_features + upd
    edge_index = jnp.stack([src, dst])
    h = jnp.maximum(_layernorm(x, axis=-1), 0.0)
    x = x + _L0_gnn_ref(h, edge_index, edge_attr_4, node_vec1, L0_gnn_Wm_ss, L0_gnn_Wm_vv, L0_gnn_Wm_sv, L0_gnn_Wm_vs, L0_gnn_Lm_s, L0_gnn_Lm_v, L0_gnn_Wu_ss, L0_gnn_Wu_vv, L0_gnn_Wu_sv, L0_gnn_Wu_vs, L0_gnn_Lu_s, L0_gnn_Lu_v)
    return x

_drawn_inputs = setup_inputs


def setup_inputs(seed=0):
    import zlib

    import numpy as np

    out = dict(_drawn_inputs(seed))
    spreads = {}
    factors = {}
    for name, (base, spread) in spreads.items():
        noise = np.random.default_rng([zlib.crc32(name.encode()), seed]).standard_normal(out[name].shape)
        drawn = base * np.exp(spread * noise) if base else spread * noise
        out[name] = jnp.asarray(drawn.astype(out[name].dtype))
    for name, factor in factors.items():
        out[name] = (out[name] * factor).astype(out[name].dtype)
    return out
```

```python
from contextlib import ExitStack

import concourse.bass as bass
from concourse import mybir

F32 = mybir.dt.float32
F32R = mybir.dt.float32r
I32 = mybir.dt.int32
ALU = mybir.AluOpType
ACT = mybir.ActivationFunctionType

S, V, C3 = 64, 32, 3
D = S + C3 * V
R = 125
SUB = 4
T = R * SUB
EPS = 1e-5
INV_SQRT3 = 0.5773502691896258
INV8 = 0.125
INV_SQRT32 = 0.17677669529663687
INV64 = 0.015625
INV32 = 0.03125
INV_SQRT2048 = 0.022097086912079608

JS, KS = 8, 4
JV, KV = 2, 4
KW = V // 4
KS_DVE = 2
JG = 4

HL = 3 * 128


def program(nc, x, src, dst, attr, consts, weights, out):
    N = x.shape[0]
    E = src.shape[0]
    NT, ET = N // T, E // T
    assert NT * T == N and ET * T == E and NT % 2 == 0 and ET % 2 == 0 and NT >= 4 and ET >= 4

    agg = nc.dram_tensor("agg", [N + T, D], F32).ap()

    x_t = x.rearrange("(t p j) f -> t p j f", p=R, j=SUB)
    out_t = out.rearrange("(t p j) f -> t p j f", p=R, j=SUB)
    agg_t = agg.rearrange("(t p j) f -> t p j f", p=R, j=SUB)
    src_col = src.rearrange("(t p j) -> t p j", p=R, j=SUB)
    src_row = src.rearrange("(t o e) -> t o e", o=1, e=T)
    dst_col = dst.rearrange("(t p j) -> t p j", p=R, j=SUB)
    attr_t = attr.rearrange("(t p j) f -> t p j f", p=R, j=SUB)

    with ExitStack() as whole:
        def keep(name, shape, dt=F32):
            return whole.enter_context(nc.sbuf_tensor(name, shape, dt))

        ident = keep("ident", [128, 128])
        edge_w = keep("edge_w", [128, 544])
        w_ss = keep("w_ss", [128, JS * KS, S])
        w_vv = keep("w_vv", [128, JV * KV, S])
        w_sv = keep("w_sv", [128, 2, KW * 128], F32R)
        w_vs = keep("w_vs", [128, 2, KW * 128], F32R)
        rot = keep("rot", [128, JS + KS + 2 * JV + 2 * KV, 128], F32R)
        rot_s_a = [rot[:, j, :] for j in range(JS)]
        rot_s_b = [rot[:, JS + k, :] for k in range(KS)]
        rot_v_a = [[rot[:, JS + KS + q * JV + j, :] for j in range(JV)] for q in range(2)]
        rot_v_b = [[rot[:, JS + KS + 2 * JV + q * KV + k, :] for k in range(KV)] for q in range(2)]
        sum_w = keep("sum_w", [128, KW, V])
        lin_s = keep("lin_s", [128, 2, 128], F32R)
        lin_v = keep("lin_v", [128, V])
        back_s = keep("back_s", [128, S])
        back_v = keep("back_v", [C3 * V, C3 * V])
        with ExitStack() as ctx:
            setup(nc, ctx, agg, N, consts, weights, ident, edge_w, w_ss, w_vv, w_sv, w_vs, rot, sum_w,
                  lin_s, lin_v, back_s, back_v)
        with ExitStack() as ctx:
            edges(nc, ctx, N, ET, x, src_col, src_row, dst_col, attr_t, consts, agg, ident, edge_w)
        with ExitStack() as ctx:
            nodes(nc, ctx, NT, x_t, agg_t, out_t, ident, w_ss, w_vv, w_sv, w_vs,
                  rot_s_a, rot_s_b, rot_v_a, rot_v_b, sum_w, lin_s, lin_v, back_s, back_v)


def setup(nc, ctx, agg, N, consts, weights, ident, edge_w, w_ss, w_vv, w_sv, w_vs, rot, sum_w,
          lin_s, lin_v, back_s, back_v):
    rot_raw = ctx.enter_context(nc.sbuf_tensor("rot_raw", [128, rot.shape[1], 128], F32))
    sv_raw = ctx.enter_context(nc.sbuf_tensor("sv_raw", [128, KW * 128], F32))
    vs_raw = ctx.enter_context(nc.sbuf_tensor("vs_raw", [128, KW * 128], F32))
    lin_raw = ctx.enter_context(nc.sbuf_tensor("lin_raw", [128, 128], F32))
    lin_s_eye = ctx.enter_context(nc.sbuf_tensor("lin_s_eye", [128, 128], F32))
    lin_v_eye = ctx.enter_context(nc.sbuf_tensor("lin_v_eye", [128, V], F32))
    zeros = ctx.enter_context(nc.sbuf_tensor("zeros", [R, 4 * SUB * D], F32))
    loaded = ctx.enter_context(nc.semaphore("weights_loaded"))
    cleared = ctx.enter_context(nc.semaphore("zeros_made"))
    table_zero = ctx.enter_context(nc.semaphore("table_zero"))
    scaled = ctx.enter_context(nc.semaphore("weights_scaled"))
    high = ctx.enter_context(nc.semaphore("weights_high"))
    block = ctx.enter_context(nc.Block("setup"))

    loads = [(ident[:, :], consts["ident"]), (edge_w[:, :], weights["edge_w"]),
             (w_ss[:, :, :], weights["w_ss"]), (w_vv[:, :, :], weights["w_vv"]),
             (sv_raw[:, :], weights["w_sv"]), (vs_raw[:, :], weights["w_vs"]),
             (rot_raw[:, :, :], consts["rot"]), (sum_w[:, :, :], consts["sum_w"]),
             (lin_raw[:, :], weights["lin_s"]), (lin_v[:, :], weights["lin_v"]),
             (lin_s_eye[:, :], consts["lin_s_eye"]), (lin_v_eye[:, :], consts["lin_v_eye"]),
             (back_s[:, :], consts["back_s"]), (back_v[:, :], consts["back_v"])]
    splits = ((lin_raw, lin_s), (sv_raw, w_sv), (vs_raw, w_vs))
    rows = N + T
    wide = rows // T // 4
    rest = rows - wide * 4 * T

    @block.sync
    def _(sp):
        for to, frm in loads:
            sp.dma_start(to, frm).then_inc(loaded, 16)
        sp.wait_ge(cleared, 1)
        big = agg[0:wide * 4 * T, :].rearrange("(t p j) f -> t p (j f)", p=R, j=4 * SUB)
        with sp.Fori(0, wide) as t:
            sp.dma_start(big[t], zeros[:, :]).then_inc(table_zero, 16)
        if rest:
            sp.dma_start(agg[wide * 4 * T:rows, :].rearrange("(p j) f -> p (j f)", p=R),
                         zeros[:, 0:rest // R * D]).then_inc(table_zero, 16)
        sp.wait_ge(table_zero, 16 * (wide + (1 if rest else 0)))

    @block.vector
    def _(dve):
        dve.memset(zeros[:, :], 0.0).then_inc(cleared, 1)
        dve.wait_ge(loaded, 16 * len(loads))
        dve.scalar_tensor_tensor(out=lin_raw[:, :], in0=lin_raw[:, :], scalar=INV8, in1=lin_s_eye[:, :],
                                 op0=ALU.mult, op1=ALU.add).then_inc(scaled, 1)
        dve.scalar_tensor_tensor(out=lin_v[:, :], in0=lin_v[:, :], scalar=INV_SQRT32, in1=lin_v_eye[:, :],
                                 op0=ALU.mult, op1=ALU.add)
        dve.tensor_scalar(w_ss[:, :, :], w_ss[:, :, :], INV64, None, ALU.mult)
        dve.tensor_scalar(w_vv[:, :, :], w_vv[:, :, :], INV_SQRT3 * INV32, None, ALU.mult)
        for a, b, f in EDGE_FACTORS:
            dve.tensor_scalar(edge_w[:, a:b], edge_w[:, a:b], f, None, ALU.mult)
        for raw in (sv_raw, vs_raw):
            dve.tensor_scalar(raw[:, :], raw[:, :], INV_SQRT2048, None, ALU.mult).then_inc(scaled, 1)
        for n, (raw, w) in enumerate(splits):
            dve.wait_ge(high, n + 1)
            dve.tensor_tensor(w[:, 1, :], raw[:, :], w[:, 0, :].bitcast(F32), ALU.subtract)

    @block.scalar
    def _(act):
        act.wait_ge(loaded, 16 * len(loads))
        act.activation(rot[:, :, :], rot_raw[:, :, :], ACT.Copy)
        for n, (raw, w) in enumerate(splits):
            act.wait_ge(scaled, n + 1)
            act.activation(w[:, 0, :], raw[:, :], ACT.Copy).then_inc(high, 1)


EDGE_FACTORS = [(0, 64, INV8), (64, 128, INV_SQRT32), (128, 192, INV8), (192, 256, INV_SQRT32),
                (256, 384, INV_SQRT3 * INV_SQRT32), (384, 416, INV8),
                (416, 480, INV_SQRT32), (480, 544, INV_SQRT3 * INV_SQRT32)]
VV_AT = (0, 64, 160)
SV_AT = 128


def edges(nc, ctx, N, ET, x, src_col, src_row, dst_col, attr_t, consts, agg, ident, edge_w):
    def sb(name, shape, dt=F32):
        return ctx.enter_context(nc.sbuf_tensor(name, shape, dt))

    def sem(name):
        return ctx.enter_context(nc.semaphore(name))

    dst_i = [sb(f"dst_i{u}", [R, SUB], I32) for u in range(2)]
    src_i = [sb(f"src_i{u}", [R, SUB], I32) for u in range(2)]
    row_i = [sb(f"row_i{u}", [R, T], I32) for u in range(2)]
    at = [sb(f"at{u}", [R, SUB, 4]) for u in range(2)]
    xg = [sb(f"xg{u}", [R, SUB, D]) for u in range(2)]
    hg = [sb(f"hg{u}", [R, SUB, D]) for u in range(2)]
    stats = sb("stats", [R, SUB, 6])
    mean_var = sb("mean_var", [R, SUB, 2])
    std = sb("std", [R, SUB])
    var_eps = sb("var_eps", [R, SUB])
    rstd = [sb(f"rstd{u}", [R, SUB]) for u in range(2)]
    shift = [sb(f"shift{u}", [R, SUB]) for u in range(2)]
    turned = [sb(f"turned{u}", [128, 2, T]) for u in range(2)]
    msg = [sb(f"msg{u}", [R, SUB, D + SUB]) for u in range(2)]
    row_f = [sb(f"row_f{u}", [R, T]) for u in range(2)]
    col_f = [sb(f"col_f{u}", [R, SUB]) for u in range(2)]
    same = [sb(f"same{u}", [R, SUB, T]) for u in range(2)]
    before = sb("before", [R, R])
    seen = sb("seen", [R, SUB, R])
    own = [sb(f"own{u}", [R, SUB]) for u in range(2)]
    rank = sb("rank", [R, SUB])
    spare = sb("spare", [R, SUB])
    to_spare = [sb(f"to_spare{u}", [R, SUB]) for u in range(2)]
    to_f = sb("to_f", [R, SUB])
    to_i = [sb(f"to_i{u}", [R, SUB], I32) for u in range(2)]
    total = [sb(f"total{u}", [R, SUB, D + SUB]) for u in range(2)]

    tr = ctx.enter_context(nc.psum_tensor("tr", [128, 2, 512], F32))
    lin = [ctx.enter_context(nc.psum_tensor(f"lin{u}", [128, 512], F32)) for u in range(2)]
    prod = [ctx.enter_context(nc.psum_tensor(f"prod{u}", [128, 512], F32)) for u in range(2)]
    acc = ctx.enter_context(nc.psum_tensor("acc", [128, SUB, 256], F32))

    consts_in = sem("edge_consts_in")
    dst_in = [sem(f"dst_in{u}") for u in range(2)]
    src_in = [sem(f"src_in{u}") for u in range(2)]
    gathered = [sem(f"gathered{u}") for u in range(2)]
    var_ready = sem("var_ready")
    std_ready = sem("std_ready")
    scale_ready = sem("scale_ready")
    h_ready = sem("h_ready")
    turned_psum = sem("turned_psum")
    turned_ready = sem("turned_ready")
    prod_ready = sem("prod_ready")
    lin_ready = sem("lin_ready")
    msg_ready = sem("msg_ready")
    prod_used = sem("prod_used")
    keys_ready = sem("keys_ready")
    same_ready = sem("same_ready")
    summed = sem("summed")
    total_ready = sem("total_ready")
    index_ready = sem("index_ready")
    added = sem("added")
    scale_step = sem("edge_scale_step")
    msg_step = sem("edge_msg_step")
    key_step = sem("edge_key_step")
    index_step = sem("edge_index_step")
    passed = sem("edge_waits_passed")
    passed_dve = sem("edge_vector_waits_passed")
    passed_sp = sem("edge_loads_waits_passed")
    block = ctx.enter_context(nc.Block("edges"))

    def is0(n):
        return isinstance(n, int) and n == 0

    def under2(n):
        return isinstance(n, int) and n < 2

    def rounds(eng, body):
        for n in range(4):
            body(n, n % 2)
        with eng.Fori(2, ET // 2) as i:
            for u in range(2):
                body(i * 2 + u, u)
        for n in range(ET, ET + 2):
            body(n, n % 2)

    def runs(n):
        return not isinstance(n, int) or 0 <= n < ET

    @block.sync
    def _(sp):
        sp.dma_start(before[:, :], consts["before"]).then_inc(consts_in, 16)
        sp.dma_start(spare[:, :], consts["spare"]).then_inc(consts_in, 16)

        def load(n, u):
            if not runs(n):
                return
            if not under2(n):
                sp.wait_ge(gathered[u], (n - u) * 32)
            sp.dma_start(dst_i[u][:, :], dst_col[n]).then_inc(dst_in[u], 16)
            if not under2(n):
                sp.wait_ge(keys_ready, n - 1)
                sp.sem_inc(passed_sp, 1)
                sp.wait_ge(msg_ready, (n - 1) * SUB)
            sp.dma_start(src_i[u][:, :], src_col[n]).then_inc(src_in[u], 16)
            sp.dma_start(row_i[u][:, :], src_row[n].broadcast_to((R, T))).then_inc(src_in[u], 16)
            sp.dma_start(at[u][:, :, :], attr_t[n]).then_inc(src_in[u], 16)

        rounds(sp, load)

    @block.gpsimd
    def _(pool):
        def started():
            pool.sem_inc(passed, 1)

        def gather(n, u):
            pool.wait_ge(dst_in[u], (n - u) * 8 + 16)
            if not under2(n):
                pool.wait_ge(h_ready, n - 1)
            started()
            for a in range(SUB):
                pool.indirect_dma_start(xg[u][:, a, :], None, x,
                                        bass.IndirectOffsetOnAxis(ap=dst_i[u][:, a:a + 1], axis=0))\
                    .then_inc(gathered[u], 16)

        def scatter(n, u):
            pool.wait_ge(total_ready, n + 1)
            pool.wait_ge(index_ready, n + 1)
            if not is0(n):
                pool.wait_ge(added, n * 16 * SUB)
            started()
            for a in range(SUB):
                pool.indirect_dma_start(agg, bass.IndirectOffsetOnAxis(ap=to_i[u][:, a:a + 1], axis=0),
                                        total[u][:, a, 0:D], None, compute_op=ALU.add)\
                    .then_inc(added, 16)

        gather(0, 0)

        def body(n, u):
            if not (isinstance(n, int) and n + 1 >= ET):
                gather(n + 1, 1 - u)
            if not (isinstance(n, int) and n < 2):
                scatter(n - 2, u)

        for n in range(4):
            body(n, n % 2)
        with pool.Fori(2, ET // 2 - 1) as i:
            for u in range(2):
                body(i * 2 + u, u)
        for n in range(ET - 2, ET + 2):
            body(n, n % 2)
        pool.wait_ge(added, ET * 16 * SUB)

    @block.vector
    def _(dve):
        for u in range(2):
            for b in range(SUB):
                nc.vector.memset(msg[u][:, b, D:D + b + 1], 0.0)
                if b < SUB - 1:
                    nc.vector.memset(msg[u][:, b, D + b + 1:D + SUB], 1.0)
        dve.wait_ge(consts_in, 32)

        def scales(n, u):
            dve.wait_ge(gathered[u], (n - u) * 32 + 16 * SUB)
            for a in range(SUB):
                nc.vector.bn_stats(stats[:, a, :], xg[u][:, a, :]).then_inc(scale_step, 1)
            dve.wait_ge(scale_step, n * 9 + 4)
            dve.sem_inc(passed_dve, 1)
            for a in range(SUB):
                nc.vector.bn_aggr(mean_var[:, a, :], stats[:, a, :]).then_inc(scale_step, 1)
            dve.wait_ge(scale_step, n * 9 + 8)
            nc.vector.tensor_scalar(var_eps[:, :], mean_var[:, :, 1], EPS, None, ALU.add).then_inc(var_ready, 1)

        def scales_end(n, u):
            dve.wait_ge(std_ready, n + 1)
            if not under2(n):
                dve.wait_ge(h_ready, n - 1)
            nc.vector.reciprocal(rstd[u][:, :], std[:, :]).then_inc(scale_step, 1)
            dve.wait_ge(scale_step, n * 9 + 9)
            nc.vector.scalar_tensor_tensor(out=shift[u][:, :], in0=mean_var[:, :, 0], scalar=-1.0,
                                           in1=rstd[u][:, :], op0=ALU.mult, op1=ALU.mult).then_inc(scale_ready, 1)

        def keys(n, u):
            dve.wait_ge(keys_ready, n + 1)
            if not under2(n):
                dve.wait_ge(summed, n - 1)
            for b in range(SUB):
                ins = nc.vector.tensor_scalar(same[u][:, b, :], row_f[u][:, :], col_f[u][:, b:b + 1], None,
                                              ALU.is_equal)
            ins.then_inc(same_ready, 1)
            for b in range(SUB):
                nc.vector.scalar_tensor_tensor(out=seen[:, b, :], in0=row_f[u][:, b:T:SUB],
                                               scalar=col_f[u][:, b:b + 1], in1=before[:, :],
                                               op0=ALU.is_equal, op1=ALU.mult,
                                               accum_out=own[u][:, b:b + 1]).then_inc(key_step, 1)
            nc.vector.tensor_tensor(to_spare[u][:, :], spare[:, :], col_f[u][:, :], ALU.subtract)\
                .then_inc(key_step, 1)

        def index(n, u):
            dve.wait_ge(total_ready, n + 1)
            dve.wait_ge(key_step, n * 5 + 5)
            flat = total[u][:, :, :].rearrange("p a f -> p (a f)")
            counts = flat[:, D:D + (D + SUB + 1) * (SUB - 1) + 1:D + SUB + 1]
            nc.vector.tensor_tensor(rank[:, :], own[u][:, :], counts,
                                    ALU.add).then_inc(index_step, 1)
            dve.wait_ge(index_step, n * 2 + 1)
            nc.vector.scalar_tensor_tensor(out=to_f[:, :], in0=rank[:, :], scalar=1.0, in1=to_spare[u][:, :],
                                           op0=ALU.min, op1=ALU.mult).then_inc(index_step, 1)
            dve.wait_ge(index_step, n * 2 + 2)
            if not under2(n):
                dve.wait_ge(added, (n - 1) * 16 * SUB)
            nc.vector.tensor_tensor(to_i[u][:, :], to_f[:, :], col_f[u][:, :], ALU.add).then_inc(index_ready, 1)

        def messages(n, u, pair):
            if pair == 0:
                dve.wait_ge(src_in[u], (n - u) * 24 + 48)
            base = n * 12 + pair * 6
            groups = (2 * pair, 2 * pair + 1)
            done = 0

            def vv(a, c):
                m = msg[u][:, a, 0:S]
                return nc.vector.scalar_tensor_tensor(
                    out=m, in0=prod[a % 2][0:R, VV_AT[c]:VV_AT[c] + S], scalar=at[u][:, a, c:c + 1], in1=m,
                    op0=ALU.mult, op1=ALU.add)

            for a in groups:
                m = msg[u][:, a, 0:D]
                dve.wait_ge(lin_ready, n * SUB + a + 1)
                nc.vector.scalar_tensor_tensor(out=m, in0=lin[a % 2][0:R, D:2 * D], scalar=at[u][:, a, 3:4], in1=m,
                                               op0=ALU.mult, op1=ALU.add).then_inc(msg_step, 1)
            for a in groups:
                done += 1
                dve.wait_ge(msg_step, base + done)
                vv(a, 0).then_inc(msg_step, 1)
            for a in groups:
                for c in range(C3):
                    m = msg[u][:, a, S + V * c:S + V * c + V]
                    nc.vector.scalar_tensor_tensor(out=m, in0=prod[a % 2][0:R, SV_AT:SV_AT + V],
                                                   scalar=at[u][:, a, c:c + 1], in1=m, op0=ALU.mult, op1=ALU.add)
            for a in groups:
                done += 1
                dve.wait_ge(msg_step, base + done)
                vv(a, 1).then_inc(msg_step, 1)
            for a in groups:
                done += 1
                dve.wait_ge(msg_step, base + done)
                vv(a, 2).then_inc(msg_ready, 1)

        def body(n, u):
            if runs(n):
                scales(n, u)
            if runs(n - 1):
                keys(n - 1, 1 - u)
            if runs(n):
                scales_end(n, u)
            if runs(n - 1):
                messages(n - 1, 1 - u, 0)
            if runs(n - 2):
                index(n - 2, u)
            if runs(n - 1):
                messages(n - 1, 1 - u, 1)

        rounds(dve, body)

    @block.scalar
    def _(act):
        def root(n, u):
            act.wait_ge(var_ready, n + 1)
            if not is0(n):
                act.wait_ge(scale_ready, n)
            nc.scalar.activation(std[:, :], var_eps[:, :], ACT.Sqrt).then_inc(std_ready, 1)

        def relu(n, u):
            act.wait_ge(scale_ready, n + 1)
            if not under2(n):
                act.wait_ge(turned_psum, n - 1)
            for a in range(SUB):
                sc, sh = rstd[u][:, a:a + 1], shift[u][:, a:a + 1]
                nc.scalar.activation(hg[u][:, a, 0:S], xg[u][:, a, 0:S], ACT.Relu, bias=sh, scale=sc)
                ins = nc.scalar.activation(hg[u][:, a, S:D].rearrange("p (c v) -> p c v", c=C3),
                                           xg[u][:, a, S:D].rearrange("p (v c) -> p c v", c=C3),
                                           ACT.Relu, bias=sh, scale=sc)
            ins.then_inc(h_ready, 1)

        def turned_out(n, u):
            act.wait_ge(turned_psum, n + 1)
            if not under2(n):
                act.wait_ge(prod_ready, (n - 1) * SUB)
            nc.scalar.activation(turned[u][:, :, :], tr[:, :, 0:T], ACT.Copy).then_inc(turned_ready, 1)

        def linear(n, u, pair):
            if pair == 0 and not under2(n):
                act.wait_ge(summed, n - 1)
            for a in (2 * pair, 2 * pair + 1):
                act.wait_ge(prod_ready, n * SUB + a + 1)
                nc.scalar.activation(msg[u][:, a, 0:D], lin[a % 2][0:R, 0:D], ACT.Copy).then_inc(lin_ready, 1)

        def sum_out(n, u):
            act.wait_ge(summed, n + 1)
            if not under2(n):
                act.wait_ge(added, (n - 1) * 16 * SUB)
            nc.scalar.activation(total[u][:, :, :], acc[0:R, :, 0:D + SUB], ACT.Copy).then_inc(total_ready, 1)

        def to_float(n, u):
            act.wait_ge(src_in[u], (n - u) * 24 + 48)
            if not under2(n):
                act.wait_ge(index_ready, n - 1)
            nc.scalar.activation(col_f[u][:, :], src_i[u][:, :], ACT.Copy)
            nc.scalar.activation(row_f[u][:, :], row_i[u][:, :], ACT.Copy).then_inc(keys_ready, 1)

        def body(n, u):
            if runs(n - 1):
                linear(n - 1, 1 - u, 0)
            if runs(n):
                root(n, u)
                relu(n, u)
            if runs(n - 2):
                sum_out(n - 2, u)
            if runs(n - 1):
                linear(n - 1, 1 - u, 1)
            if runs(n):
                turned_out(n, u)
                to_float(n, u)

        rounds(act, body)

    @block.tensor
    def _(pe):
        def turn(n, u):
            pe.wait_ge(h_ready, n + 1)
            if not is0(n):
                pe.wait_ge(turned_ready, n)
            for q, c in enumerate((0, V)):
                for a in range(SUB):
                    ins = nc.tensor.transpose(tr[:, q, R * a:R * a + R], hg[u][:, a, c:c + 128], ident[0:R, 0:R])
            ins.then_inc(turned_psum, 1)

        def products(n, u, pair):
            if pair == 0:
                pe.wait_ge(turned_ready, n + 1)
            for a in (2 * pair, 2 * pair + 1):
                q = a % 2
                if not (is0(n) and a < 2):
                    pe.wait_ge(msg_ready, n * SUB + a - 1)
                t1 = turned[u][:, 0, R * a:R * a + R]
                t2 = turned[u][:, 1, R * a:R * a + R]
                l2 = lin[q][0:R, 0:2 * D].rearrange("p (g f) -> p g f", g=2)
                nc.tensor.matmul(l2[:, :, 0:128], t1, edge_w[:, 0:256], start=True, stop=True)
                nc.tensor.matmul(prod[q][0:R, 0:160], t1, edge_w[:, 256:416], start=True, stop=True)
                nc.tensor.matmul(l2[:, :, 128:D], t2, edge_w[:, 416:480], start=True, stop=True)
                nc.tensor.matmul(prod[q][0:R, 160:224], t2, edge_w[:, 480:544], start=True, stop=True)\
                    .then_inc(prod_ready, 1)

        def sums(n, u):
            pe.wait_ge(msg_ready, n * SUB + SUB)
            pe.wait_ge(same_ready, n + 1)
            if not is0(n):
                pe.wait_ge(total_ready, n)
            for a in range(SUB):
                for b in range(SUB):
                    ins = nc.tensor.matmul(acc[0:R, a, 0:D + SUB], same[u][:, b, a:T:SUB], msg[u][:, b, :],
                                           start=(b == 0), stop=(b == SUB - 1))
            ins.then_inc(summed, 1)

        def body(n, u):
            if runs(n - 1):
                products(n - 1, 1 - u, 0)
            if runs(n - 2):
                sums(n - 2, u)
            if runs(n - 1):
                products(n - 1, 1 - u, 1)
            if runs(n):
                turn(n, u)

        rounds(pe, body)


def nodes(nc, ctx, NT, x_t, agg_t, out_t, ident, w_ss, w_vv, w_sv, w_vs,
          rot_s_a, rot_s_b, rot_v_a, rot_v_b, sum_w, lin_s, lin_v, back_s, back_v):
    def sb(name, shape, dt=F32):
        return ctx.enter_context(nc.sbuf_tensor(name, shape, dt))

    def sem(name):
        return ctx.enter_context(nc.semaphore(name))

    X = [sb(f"X{u}", [R, SUB, D]) for u in range(2)]
    A = sb("A", [R, SUB, D])
    H = sb("H", [R, SUB, D])
    hl = sb("hl", [R, SUB, HL])
    O = sb("O", [R, SUB, D])
    stats = sb("nstats", [R, SUB, 6])
    mean_var = sb("nmean_var", [R, SUB, 2])
    std = sb("nstd", [R, SUB])
    var_eps = sb("nvar_eps", [R, SUB])
    rstd = sb("nrstd", [R, SUB])
    shift = sb("nshift", [R, SUB])
    parts = [[sb(f"parts{u}_{q}", [128, 3, T], F32R) for q in range(2)] for u in range(2)]
    s_a = sb("s_a", [128, JS, T])
    s_b = sb("s_b", [128, KS - KS_DVE, T])
    v_a = [sb(f"v_a{u}", [128, C3, JV, T]) for u in range(2)]
    v_b = [sb(f"v_b{u}", [128, C3, T]) for u in range(2)]
    NP = 3
    P = [sb(f"P{r}", [128, JG, T]) for r in range(NP)]
    VP = [sb(f"VP{r}", [128, C3, JV, T]) for r in range(2)]
    G = sb("G", [128, JG, T])
    u0 = sb("u0", [128, T])
    u1 = sb("u1", [C3 * V, T])

    U0 = ctx.enter_context(nc.psum_tensor("U0", [128, 512], F32))
    U1 = ctx.enter_context(nc.psum_tensor("U1", [128, 512], F32))
    NR = 4
    ring = [ctx.enter_context(nc.psum_tensor(f"ring{r}", [128, 512], F32)) for r in range(NR)]
    prep = ctx.enter_context(nc.psum_tensor("prep", [128, 2, 512], F32))

    x_in = [sem(f"x_in{u}") for u in range(2)]
    a_in = sem("a_in")
    pad_ready = sem("pad_ready")
    var_ready = sem("nvar_ready")
    std_ready = sem("nstd_ready")
    scale_ready = sem("nscale_ready")
    h_ready = sem("nh_ready")
    hi_ready = sem("hi_ready")
    hl_ready = sem("hl_ready")
    prep_ready = sem("prep_ready")
    prep_used = sem("prep_used")
    source_ready = sem("source_ready")
    made = sem("made")
    made_g = sem("made_g")
    half_added = sem("half_added")
    added_v = sem("added_v")
    taken = sem("taken")
    taken_g = sem("taken_g")
    taken_v = sem("taken_v")
    u_out = sem("u_out")
    back_ready = sem("back_ready")
    out_made = sem("out_made")
    stored = sem("stored")
    step = sem("node_vector_step")
    passed_dve = sem("node_vector_waits_passed")
    block = ctx.enter_context(nc.Block("nodes"))

    def vv(k):
        return [("vv", k, c) for c in range(C3)]

    def sv(k):
        return [("sv", k, 0), ("vs", k, 0)]

    chunks = (vv(0) + sv(0) + [("ss", 0, 0)] + sv(1) + [("ss", 0, JG)] + vv(1) + sv(2) + [("ss", 1, 0)]
              + sv(3) + [("ss", 1, JG)] + vv(2) + sv(4) + sv(5) + vv(3) + sv(6) + sv(7))
    NCH = len(chunks)
    p_before = [sum(ch[0] != "vv" for ch in chunks[:n]) for n in range(NCH + 1)]
    NPC = p_before[NCH]
    vv_at = [max(n for n, ch in enumerate(chunks) if ch[:2] == ("vv", k)) for k in range(KV)]
    chunks_g = [(k, j0) for k in range(KS_DVE, KS) for j0 in range(0, JS, JG)]
    NG = len(chunks_g)
    order_g = [("split", 0), ("g", 0), ("v", 0), ("g", 1), ("split", 1), ("v", 1), ("g", 2), ("g", 3),
               ("v", 2), ("v", 3)]
    after = {5: [("g", 0)], 7: [("v", 0)], 11: [("g", 1)], 14: [("v", 1)], 17: [("g", 2)], 20: [("g", 3)],
             24: [("v", 2)], NCH - 1: [("v", 3)]}
    prep_steps = [("turn", 1, g) for g in range(3)]
    prep_steps += [("v_b", c, 0) for c in range(C3)]
    prep_steps += [("turn", 0, g) for g in range(3)]
    prep_steps += [("v_a", c, j) for c in range(C3) for j in range(JV)]
    prep_steps += [("s_b", k, 0) for k in range(KS_DVE, KS)]
    prep_steps += [("s_a", j, 0) for j in range(JS)]
    NPREP = len(prep_steps)
    prep_after = [3, 3, 4, 5, 6, 7] + [13 + n for n in range(NPREP - 6)]
    TURNED_SUMS, TURNED_H = 3, 9
    FIRST_S = prep_steps.index(("s_b", KS_DVE, 0))
    BACK, FINISH, SCALES, SCALES_END = 1, 2, 6, 8

    def tiles(eng, body):
        for t in range(2):
            body(t, t, False)
        with eng.Fori(1, NT // 2 - 1) as i:
            for u in range(2):
                body(i * 2 + u, u, False)
        for t in range(NT - 2, NT):
            body(t, t % 2, t == NT - 1)

    def is0(t):
        return isinstance(t, int) and t == 0

    @block.sync
    def _(sp):
        def load(t, u):
            if not is0(t):
                sp.wait_ge(hl_ready, t * 2 - 1)
            sp.dma_start(A[:, :, :], agg_t[t]).then_inc(a_in, 16)
            if not (isinstance(t, int) and t < 2):
                sp.wait_ge(out_made, t - 1)
            sp.dma_start(X[u][:, :, :], x_t[t]).then_inc(x_in[u], 16)

        def store(t):
            sp.wait_ge(out_made, t + 1)
            sp.dma_start(out_t[t], O[:, :, :]).then_inc(stored, 16)

        load(0, 0)
        load(1, 1)

        def body(t, u, last):
            if not is0(t):
                if not last:
                    load(t + 1, 1 - u)
                store(t - 1)

        tiles(sp, body)
        store(NT - 1)
        sp.wait_ge(stored, 16 * NT)

    @block.gpsimd
    def _(pool):
        pool.memset(hl[:, :, HL - 64:HL], 0.0).then_inc(pad_ready, 1)

        def split(t, q):
            frm = (A, H)[q]
            pool.wait_ge(hi_ready, t * 2 + q + 1)
            v = hl[:, :, 2 * S:2 * S + 2 * C3 * V].rearrange("p j (c g v) -> p j c g v", c=C3, g=2)
            nc.gpsimd.tensor_tensor(hl[:, :, S:2 * S].bitcast(F32R), frm[:, :, 0:S], hl[:, :, 0:S], ALU.subtract)
            nc.gpsimd.tensor_tensor(v[:, :, :, 1, :].bitcast(F32R),
                                    frm[:, :, S:D].rearrange("p j (c v) -> p j c v", c=C3), v[:, :, :, 0, :],
                                    ALU.subtract).then_inc(hl_ready, 1)

        def products(t, g):
            k, j0 = chunks_g[g]
            if g == 0:
                pool.wait_ge(prep_used, t * NPREP + NPREP)
            if not (is0(t) and g == 0):
                pool.wait_ge(taken_g, t * NG + g)
            nc.gpsimd.tensor_tensor(
                G[:, :, :], s_a[:, j0:j0 + JG, :],
                s_b[:, k - KS_DVE, :].unsqueeze(1).broadcast_to((128, JG, T)), ALU.mult).then_inc(made_g, 1)

        def add_components(t, k):
            vp = VP[k % 2]
            pool.wait_ge(made, t * NCH + vv_at[k] + 1)
            nc.gpsimd.tensor_tensor(vp[:, 0, :, :], vp[:, 0, :, :], vp[:, 1, :, :], ALU.add)\
                .then_inc(half_added, 1)
            pool.wait_ge(half_added, t * KV + k + 1)
            nc.gpsimd.tensor_tensor(vp[:, 0, :, :], vp[:, 0, :, :], vp[:, 2, :, :], ALU.add)\
                .then_inc(added_v, 1)

        split(0, 0)
        split(0, 1)

        def body(t, u, last):
            for what, n in order_g:
                if what == "g":
                    products(t, n)
                elif what == "v":
                    add_components(t, n)
                elif not last:
                    split(t + 1, n)

        tiles(pool, body)

    @block.scalar
    def _(act):
        def high(t, q):
            frm = (A, H)[q]
            v = hl[:, :, 2 * S:2 * S + 2 * C3 * V].rearrange("p j (c g v) -> p j c g v", c=C3, g=2)
            nc.scalar.activation(hl[:, :, 0:S].bitcast(F32R), frm[:, :, 0:S], ACT.Copy)
            nc.scalar.activation(v[:, :, :, 0, :].bitcast(F32R),
                                 frm[:, :, S:D].rearrange("p j (c v) -> p j c v", c=C3),
                                 ACT.Copy).then_inc(hi_ready, 1)

        def high_sums(t):
            act.wait_ge(a_in, t * 16 + 16)
            if not is0(t):
                act.wait_ge(prep_ready, (t - 1) * NPREP + TURNED_H)
            high(t, 0)

        def normalise(t, u):
            act.wait_ge(var_ready, t + 1)
            nc.scalar.activation(std[:, :], var_eps[:, :], ACT.Sqrt).then_inc(std_ready, 1)
            act.wait_ge(scale_ready, t + 1)
            if not is0(t):
                act.wait_ge(hl_ready, t * 2)
            for a in range(SUB):
                sc, sh = rstd[:, a:a + 1], shift[:, a:a + 1]
                nc.scalar.activation(H[:, a, 0:S], X[u][:, a, 0:S], ACT.Relu, bias=sh, scale=sc)
                ins = nc.scalar.activation(H[:, a, S:D].rearrange("p (c v) -> p c v", c=C3),
                                           X[u][:, a, S:D].rearrange("p (v c) -> p c v", c=C3),
                                           ACT.Relu, bias=sh, scale=sc)
            ins.then_inc(h_ready, 1)
            act.wait_ge(h_ready, t + 1)
            act.wait_ge(prep_ready, t * NPREP + TURNED_SUMS)
            high(t, 1)

        def take(t, u, n):
            what, a, b = prep_steps[n]
            if n == FIRST_S and not is0(t):
                act.wait_ge(made_g, t * NG)
            act.wait_ge(prep_ready, t * NPREP + n + 1)
            to = {"turn": lambda: parts[u][a][:, b, :], "s_a": lambda: s_a[:, a, :],
                  "s_b": lambda: s_b[:, a - KS_DVE, :], "v_a": lambda: v_a[u][:, a, b, :],
                  "v_b": lambda: v_b[u][:, a, :]}[what]()
            nc.scalar.activation(to, prep[:, n % 2, 0:T], ACT.Copy).then_inc(prep_used, 1)

        def prepare(t, u):
            high_sums(t)
            for n in range(6):
                take(t, u, n)
            normalise(t, u)
            for n in range(6, NPREP):
                take(t, u, n)

        prepare(0, 0)

        def body(t, u, last):
            if not last:
                prepare(t + 1, 1 - u)
            act.wait_ge(taken_v, (t + 1) * KV)
            if not is0(t):
                act.wait_ge(back_ready, t)
            nc.scalar.activation(u0[:, :], U0[:, 0:T], ACT.Copy)
            nc.scalar.activation(u1[:, :], U1[0:C3 * V, 0:T], ACT.Copy).then_inc(u_out, 1)

        tiles(act, body)

    @block.vector
    def _(dve):
        def scales(t, u):
            dve.wait_ge(x_in[u], (t - u) * 8 + 16)
            if not is0(t):
                dve.wait_ge(h_ready, t)
            for a in range(SUB):
                nc.vector.bn_stats(stats[:, a, :], X[u][:, a, :]).then_inc(step, 1)
            dve.wait_ge(step, t * 9 + 4)
            dve.sem_inc(passed_dve, 1)
            for a in range(SUB):
                nc.vector.bn_aggr(mean_var[:, a, :], stats[:, a, :]).then_inc(step, 1)
            dve.wait_ge(step, t * 9 + 8)
            nc.vector.tensor_scalar(var_eps[:, :], mean_var[:, :, 1], EPS, None, ALU.add).then_inc(var_ready, 1)

        def scales_end(t):
            dve.wait_ge(std_ready, t + 1)
            nc.vector.reciprocal(rstd[:, :], std[:, :]).then_inc(step, 1)
            dve.wait_ge(step, t * 9 + 9)
            nc.vector.scalar_tensor_tensor(out=shift[:, :], in0=mean_var[:, :, 0], scalar=-1.0,
                                           in1=rstd[:, :], op0=ALU.mult, op1=ALU.mult).then_inc(scale_ready, 1)

        def product(t, u, n):
            kind, k, c = chunks[n]
            dve.wait_ge(source_ready, t * NCH + n + 1)
            if n == 0:
                dve.wait_ge(prep_used, t * NPREP + FIRST_S)
            if kind == "ss":
                dve.wait_ge(prep_used, t * NPREP + NPREP)
            p = P[p_before[n] % NP]
            if kind == "vv":
                if c == 0 and not (is0(t) and k < 2):
                    dve.wait_ge(taken_v, t * KV + k - 1)
                out, b = VP[k % 2][:, c, :, :], v_a[u][:, c, :, :]
            else:
                before_it = reuse[n]
                if before_it is not None and not (is0(t) and before_it < 0):
                    dve.wait_ge(taken, t * NPC + before_it + 1)
                if kind == "ss":
                    out, b = p[:, 0:JG, :], s_a[:, c:c + JG, :]
                elif kind == "sv":
                    out, b = p[:, 0:C3, :], v_b[u][:, :, :]
                else:
                    out, b = p[:, 0:C3, :], v_a[u][:, :, 0, :]
            nc.vector.tensor_tensor(out, ring[n % NR][:, 0:T].unsqueeze(1).broadcast_to((128, out.shape[1], T)), b,
                                    ALU.mult).then_inc(made, 1)

        reuse = []
        for n in range(NCH):
            m = p_before[n]
            same = [q for q in range(-NPC, m) if (q + NPC if q < 0 else q) % NP == m % NP]
            reuse.append(max(same))

        def finish(t, u):
            dve.wait_ge(back_ready, t + 1)
            if not is0(t):
                dve.wait_ge(stored, t * 16)
            nc.vector.tensor_tensor(O[:, :, :], X[u][:, :, :], prep[0:R, :, :].rearrange(
                "p b (h f) -> p (b h) f", h=2)[:, :, 0:D], ALU.add).then_inc(out_made, 1)

        scales(0, 0)
        scales_end(0)

        def body(t, u, last):
            for n in range(NCH):
                product(t, u, n)
                if n == FINISH and not is0(t):
                    finish(t - 1, 1 - u)
                if n == SCALES and not last:
                    scales(t + 1, 1 - u)
                if n == SCALES_END and not last:
                    scales_end(t + 1)

        tiles(dve, body)
        finish(NT - 1, (NT - 1) % 2)

    @block.tensor
    def _(pe):
        pe.wait_ge(pad_ready, 1)

        def rotate(to, u, q, c, sel):
            if c is None:
                return nc.tensor.matmul(to, sel, parts[u][q][:, 0, :], start=True, stop=True)
            return nc.tensor.matmul(to, sel[c % 2], parts[u][q][:, 1 + c // 2, :], start=True, stop=True)

        def prepare(t, u, n):
            what, a, b = prep_steps[n]
            to = prep[:, n % 2, 0:T]
            if n == 0 and not (isinstance(t, int) and t < 2):
                pe.wait_ge(out_made, t - 1)
            if what == "turn" and b == 0:
                pe.wait_ge(hl_ready, t * 2 + (1 if a else 2))
            if n >= 2:
                pe.wait_ge(prep_used, t * NPREP + n - 1)
            elif not is0(t):
                pe.wait_ge(prep_used, t * NPREP)
            if n in (TURNED_SUMS, TURNED_H):
                pe.wait_ge(prep_used, t * NPREP + n)
            if what == "turn":
                for i in range(SUB):
                    ins = nc.tensor.transpose(prep[:, n % 2, R * i:R * i + R], hl[:, i, 128 * b:128 * b + 128],
                                              ident[0:R, 0:R])
            elif what == "s_a":
                ins = rotate(to, u, 0, None, rot_s_a[a])
            elif what == "s_b":
                ins = rotate(to, u, 1, None, rot_s_b[a])
            elif what == "v_a":
                ins = rotate(to, u, 0, a, [rot_v_a[q][b] for q in range(2)])
            else:
                ins = rotate(to, u, 1, a, [rot_v_b[q][0] for q in range(2)])
            ins.then_inc(prep_ready, 1)

        def source(t, u, n):
            kind, k, c = chunks[n]
            to = ring[n % NR][:, 0:T]
            if not (is0(t) and n < NR):
                pe.wait_ge(made, t * NCH + n - NR + 1)
            if kind == "ss":
                ins = rotate(to, u, 1, None, rot_s_b[k])
            elif kind == "vv":
                ins = rotate(to, u, 1, c, [rot_v_b[q][k] for q in range(2)])
            else:
                q, w = (0, w_sv) if kind == "sv" else (1, w_vs)
                for half in range(2):
                    ins = nc.tensor.matmul(to, w[:, half, 128 * k:128 * k + 128], parts[u][q][:, 0, :],
                                           start=(half == 0), stop=(half == 1))
            ins.then_inc(source_ready, 1)

        plan = [("lin_s", 0, 0, None), ("lin_v", 0, 0, None)]
        for n in range(NCH):
            if chunks[n][0] != "vv":
                plan.append((*chunks[n], "p"))
            for what, m in after.get(n, []):
                plan.append(("ss", *chunks_g[m], "g") if what == "g" else ("vv", m, 0, "v"))

        def groups(kind):
            return [0, 1] if kind in ("lin_s", "ss", "vv") else [2 + c for c in range(C3)]

        stops = {g: max(n for n, st in enumerate(plan) if g in groups(st[0])) for g in range(2 + C3)}

        def accumulate(at, u, p):
            kind, k, c, _ = plan[at]
            start = at < 2

            def add(g, w, moving, end=True):
                to = U0[S * g:S * g + S, 0:T] if g < 2 else U1[V * (g - 2):V * (g - 2) + V, 0:T]
                return nc.tensor.matmul(to, w, moving, start=start, stop=(at == stops[g] and end))

            if kind == "lin_s":
                for half in range(2):
                    ins = nc.tensor.matmul(U0[:, 0:T], lin_s[:, half, :], parts[u][0][:, 0, :],
                                           start=(half == 0), stop=False)
            elif kind == "lin_v":
                for c in range(C3):
                    ins = add(2 + c, lin_v[:, :], v_a[u][:, c, 0, :])
            elif kind in ("ss", "vv"):
                size = JG if kind == "ss" else JV
                for m in range(size):
                    w = w_ss[:, (c + m) * KS + k, :] if kind == "ss" else w_vv[:, m * KV + k, :]
                    ins = add(m % 2, w, p[:, m, :], m >= size - 2)
            else:
                for c in range(C3):
                    ins = add(2 + c, sum_w[:, k, :], p[:, c, :])
            return ins

        def back(t):
            pe.wait_ge(u_out, t + 1)
            pe.wait_ge(prep_used, NT * NPREP if isinstance(t, int) and t == NT - 1 else (t + 2) * NPREP)
            for a in range(SUB):
                to = prep[0:R, a // 2, 256 * (a % 2):256 * (a % 2) + D]
                nc.tensor.matmul(to[:, 0:S], u0[:, R * a:R * a + R], back_s[:, :], start=True, stop=True)
                ins = nc.tensor.matmul(to[:, S:D], u1[:, R * a:R * a + R], back_v[:, :], start=True, stop=True)
            ins.then_inc(back_ready, 1)

        def body(t, u, last):
            pe.wait_ge(prep_used, t * NPREP + FIRST_S)
            if is0(t):
                for n in range(3):
                    source(t, u, n)
            if not is0(t):
                pe.wait_ge(u_out, t)
            accumulate(0, u, None)
            accumulate(1, u, None)
            at = 2
            prepared = 0
            for n in range(NCH):
                if chunks[n][0] != "vv":
                    pe.wait_ge(made, t * NCH + n + 1)
                    ins = accumulate(at, u, P[p_before[n] % NP])
                    ins.then_inc(taken, 1)
                    at += 1
                for what, m in after.get(n, []):
                    if what == "g":
                        pe.wait_ge(made_g, t * NG + m + 1)
                        ins = accumulate(at, u, G).then_inc(taken_g, 1)
                    else:
                        pe.wait_ge(added_v, t * KV + m + 1)
                        ins = accumulate(at, u, VP[m % 2][:, 0, :, :]).then_inc(taken_v, 1)
                    at += 1
                for m in ahead[n]:
                    if m < NCH:
                        source(t, u, m)
                    elif not last:
                        source(t + 1, 1 - u, m - NCH)
                if n == BACK and not is0(t):
                    back(t - 1)
                while not last and prepared < NPREP and prep_after[prepared] <= n:
                    prepare(t + 1, 1 - u, prepared)
                    prepared += 1

        ahead = [[] for _ in range(NCH)]
        for n in range(0, NCH, 2):
            ahead[n] = [m for m in (n + 3, n + 4) if m < NCH + 3]

        for n in range(NPREP):
            prepare(0, 0, n)
        tiles(pe, body)
        back(NT - 1)


def shape_constants():
    import numpy as np

    r, q = np.arange(128)[:, None], np.arange(128)[None, :]
    ident = (r == q).astype(np.float32)
    rot = []
    b, l = q // S, q % S
    rot += [r % S == (l + j) % S for j in range(JS)]
    rot += [r % S == (l + 8 * k + 32 * b) % S for k in range(KS)]
    b, l = q // V, q % V
    rot += [(r // 64 == g) & (r % V == (l + j) % V) for g in range(2) for j in range(JV)]
    rot += [(r // 64 == g) & (r % V == (l + 2 * b + 8 * k) % V) for g in range(2) for k in range(KV)]
    rot = np.stack(rot, axis=1).astype(np.float32)
    w = np.arange(V)[None, None, :]
    sum_w = (w == 4 * np.arange(KW)[None, :, None] + (np.arange(128) // V)[:, None, None]).astype(np.float32)
    lin_s_eye = ((r % S == q) & (q < S)).astype(np.float32)
    lin_v_eye = np.eye(128, V, dtype=np.float32)
    back_s = (np.arange(128)[:, None] % S == np.arange(S)[None, :]).astype(np.float32)
    cv = np.arange(C3 * V)
    back_v = (C3 * (cv[:, None] % V) + cv[:, None] // V == cv[None, :]).astype(np.float32)
    before = (np.arange(R)[None, :] < np.arange(R)[:, None]).astype(np.float32)
    return {"ident": ident, "rot": rot, "sum_w": sum_w, "lin_s_eye": lin_s_eye, "lin_v_eye": lin_v_eye,
            "back_s": back_s, "back_v": back_v, "before": before}


def weight_layouts(w):
    import numpy as np

    f = np.float32
    out = {}
    q = np.arange(128)
    b, l = q // S, q % S
    out["w_ss"] = np.stack([w["Wu_ss"][(l + j) % S, (l + 8 * k + 32 * b) % S] for j in range(JS) for k in range(KS)],
                           axis=1)
    b, l = q // V, q % V
    out["w_vv"] = np.stack([w["Wu_vv"][(l + j) % V, (l + 2 * b + 8 * k) % V] for j in range(JV) for k in range(KV)],
                           axis=1)
    rows = np.arange(128)[:, None] % S
    out["w_sv"] = np.concatenate([w["Wu_sv"][rows, ((l + 2 * b) % V)[None], (4 * k + b)[None]] for k in range(KW)],
                                 axis=1)
    out["w_vs"] = np.concatenate([w["Wu_vs"][l[None], rows, (4 * k + b)[None]] for k in range(KW)], axis=1)
    out["lin_s"] = np.zeros((128, 128), f)
    out["lin_s"][0:S, 0:S] = out["lin_s"][S:2 * S, 0:S] = w["Lu_s"]
    out["lin_v"] = np.zeros((128, V), f)
    out["lin_v"][0:V] = w["Lu_v"]
    e = np.zeros((128, 544), f)
    e[0:S, 0:64], e[0:S, 128:192], e[0:S, 384:416] = w["Lm_s"], w["Wm_ss"], w["Wm_sv"]
    for c in range(2):
        rows = slice(S + V * c, S + V * c + V)
        e[rows, 64 + V * c:64 + V * c + V] = w["Lm_v"]
        e[rows, 192 + V * c:192 + V * c + V] = w["Wm_vs"]
        e[rows, 256 + S * c:256 + S * c + S] = w["Wm_vv"]
    e[96:128, 416:448], e[96:128, 448:480], e[96:128, 480:544] = w["Lm_v"], w["Wm_vs"], w["Wm_vv"]
    out["edge_w"] = e
    return {n: np.ascontiguousarray(a) for n, a in out.items()}


def kernel(x, src, dst, edge_attr_4, node_vec1, **weights):
    import numpy as np
    import concourse.bacc as bacc
    from concourse.bass_utils import run_bass_kernel_spmd

    nc = bacc.Bacc("TRN2", target_bir_lowering=False, num_devices=1)
    arrays = {}

    def take(name, a):
        arrays[name] = a = np.ascontiguousarray(a)
        return nc.dram_tensor(name, a.shape, mybir.dt.from_np(a.dtype), kind="ExternalInput").ap()

    x_ap, src_ap, dst_ap, attr_ap = (take(n, a) for n, a in
                                     (("x", x), ("src", src), ("dst", dst), ("attr", edge_attr_4)))
    consts = shape_constants()
    consts["spare"] = (x.shape[0] + SUB * np.arange(R)[:, None] + np.arange(SUB)[None, :]).astype(np.float32)
    consts = {n: take("const_" + n, a) for n, a in consts.items()}
    layouts = weight_layouts({n.removeprefix("L0_gnn_"): np.asarray(a) for n, a in weights.items()})
    layouts = {n: take("weight_" + n, a) for n, a in layouts.items()}
    out = nc.dram_tensor("out", x.shape, F32, kind="ExternalOutput").ap()
    program(nc, x_ap, src_ap, dst_ap, attr_ap, consts, layouts, out)
    return run_bass_kernel_spmd(nc, [arrays], core_ids=[0]).results[0]["out"]
```

```python
from contextlib import ExitStack

import concourse.bass as bass
from concourse import mybir

F32 = mybir.dt.float32
F32R = mybir.dt.float32r
I32 = mybir.dt.int32
ALU = mybir.AluOpType
ACT = mybir.ActivationFunctionType

S, V, C3 = 64, 32, 3
D = S + C3 * V
R = 125
SUB = 4
T = R * SUB
RE = R + R % 2
EPS = 1e-5
INV_SQRT3 = 0.5773502691896258
INV8 = 0.125
INV_SQRT32 = 0.17677669529663687
INV64 = 0.015625
INV32 = 0.03125
INV_SQRT2048 = 0.022097086912079608

JS, KS = 8, 4
JV, KV = 2, 4
KW = V // 4
SS_SIZES = (4, 4, 2, 2)
SS_DVE = sum(SS_SIZES)
KS_G = SS_DVE // JS
JG = 2

HL = 3 * 128


def program(nc, x, src, dst, attr, consts, weights, out):
    N = x.shape[0]
    E = src.shape[0]
    NT, ET = N // T, E // T
    assert NT * T == N and ET * T == E and NT % 2 == 0 and ET % 2 == 0 and NT >= 4 and ET >= 10

    agg = nc.dram_tensor("agg", [N + T, D], F32).ap()

    x_t = x.rearrange("(t p j) f -> t p j f", p=R, j=SUB)
    out_t = out.rearrange("(t p j) f -> t p j f", p=R, j=SUB)
    agg_t = agg.rearrange("(t p j) f -> t p j f", p=R, j=SUB)
    src_col = src.rearrange("(t p j) -> t p j", p=R, j=SUB)
    src_row = src.rearrange("(t o e) -> t o e", o=1, e=T)
    dst_col = dst.rearrange("(t p j) -> t p j", p=R, j=SUB)
    attr_t = attr.rearrange("(t p j) f -> t p j f", p=R, j=SUB)

    with ExitStack() as whole:
        def keep(name, shape, dt=F32):
            return whole.enter_context(nc.sbuf_tensor(name, shape, dt))

        ident = keep("ident", [128, 128])
        ident_r = keep("ident_r", [128, 128], F32R)
        edge_w = keep("edge_w", [128, 544])
        w_ss = keep("w_ss", [128, JS * KS, S])
        w_vv = keep("w_vv", [128, JV * KV, S])
        w_sv = keep("w_sv", [128, 2, KW * 128], F32R)
        w_vs = keep("w_vs", [128, 2, KW * 128], F32R)
        rot = keep("rot", [128, JS + KS + 2 * JV + 2 * KV, 128], F32R)
        rot_s_a = [rot[:, j, :] for j in range(JS)]
        rot_s_b = [rot[:, JS + k, :] for k in range(KS)]
        rot_v_a = [[rot[:, JS + KS + q * JV + j, :] for j in range(JV)] for q in range(2)]
        rot_v_b = [[rot[:, JS + KS + 2 * JV + q * KV + k, :] for k in range(KV)] for q in range(2)]
        sum_w = keep("sum_w", [128, KW, V])
        lin_s = keep("lin_s", [128, 2, 128], F32R)
        lin_v = keep("lin_v", [128, V])
        back_s = keep("back_s", [128, S])
        back_v = keep("back_v", [128, D])
        with ExitStack() as clear:
            zeros = clear.enter_context(nc.sbuf_tensor("zeros", [R, 4 * SUB * D], F32))
            table_zero = clear.enter_context(nc.semaphore("table_zero"))
            with ExitStack() as ctx:
                clears = setup(nc, ctx, agg, N, consts, weights, ident, ident_r, edge_w, w_ss, w_vv, w_sv, w_vs,
                               rot, sum_w, lin_s, lin_v, back_s, back_v, zeros, table_zero)
            with ExitStack() as ctx:
                edges(nc, ctx, N, ET, x, src_col, src_row, dst_col, attr_t, consts, agg, ident, edge_w,
                      table_zero, clears)
        with ExitStack() as ctx:
            nodes(nc, ctx, NT, x_t, agg_t, out_t, ident_r, w_ss, w_vv, w_sv, w_vs,
                  rot_s_a, rot_s_b, rot_v_a, rot_v_b, sum_w, lin_s, lin_v, back_s, back_v)


def setup(nc, ctx, agg, N, consts, weights, ident, ident_r, edge_w, w_ss, w_vv, w_sv, w_vs, rot, sum_w,
          lin_s, lin_v, back_s, back_v, zeros, table_zero):
    rot_raw = ctx.enter_context(nc.sbuf_tensor("rot_raw", [128, rot.shape[1], 128], F32))
    sv_raw = ctx.enter_context(nc.sbuf_tensor("sv_raw", [128, KW * 128], F32))
    vs_raw = ctx.enter_context(nc.sbuf_tensor("vs_raw", [128, KW * 128], F32))
    lin_raw = ctx.enter_context(nc.sbuf_tensor("lin_raw", [128, 128], F32))
    lin_s_eye = ctx.enter_context(nc.sbuf_tensor("lin_s_eye", [128, 128], F32))
    lin_v_eye = ctx.enter_context(nc.sbuf_tensor("lin_v_eye", [128, V], F32))
    loaded = ctx.enter_context(nc.semaphore("weights_loaded"))
    cleared = ctx.enter_context(nc.semaphore("zeros_made"))
    scaled = ctx.enter_context(nc.semaphore("weights_scaled"))
    high = ctx.enter_context(nc.semaphore("weights_high"))
    block = ctx.enter_context(nc.Block("setup"))

    loads = [(ident[:, :], consts["ident"]), (edge_w[:, :], weights["edge_w"]),
             (w_ss[:, :, :], weights["w_ss"]), (w_vv[:, :, :], weights["w_vv"]),
             (sv_raw[:, :], weights["w_sv"]), (vs_raw[:, :], weights["w_vs"]),
             (rot_raw[:, :, :], consts["rot"]), (sum_w[:, :, :], consts["sum_w"]),
             (lin_raw[:, :], weights["lin_s"]), (lin_v[:, :], weights["lin_v"]),
             (lin_s_eye[:, :], consts["lin_s_eye"]), (lin_v_eye[:, :], consts["lin_v_eye"]),
             (back_s[:, :], consts["back_s"]), (back_v[:, :], consts["back_v"])]
    splits = ((lin_raw, lin_s), (sv_raw, w_sv), (vs_raw, w_vs))
    rows = N + T
    wide = rows // T // 4
    rest = rows - wide * 4 * T

    @block.sync
    def _(sp):
        for to, frm in loads:
            sp.dma_start(to, frm).then_inc(loaded, 16)
        sp.wait_ge(loaded, 16 * len(loads))

    @block.vector
    def _(dve):
        dve.memset(zeros[:, :], 0.0).then_inc(cleared, 1)
        dve.wait_ge(loaded, 16 * len(loads))
        dve.scalar_tensor_tensor(out=lin_raw[:, :], in0=lin_raw[:, :], scalar=INV8, in1=lin_s_eye[:, :],
                                 op0=ALU.mult, op1=ALU.add).then_inc(scaled, 1)
        dve.scalar_tensor_tensor(out=lin_v[:, :], in0=lin_v[:, :], scalar=INV_SQRT32, in1=lin_v_eye[:, :],
                                 op0=ALU.mult, op1=ALU.add)
        dve.tensor_scalar(w_ss[:, :, :], w_ss[:, :, :], INV64, None, ALU.mult)
        dve.tensor_scalar(w_vv[:, :, :], w_vv[:, :, :], INV_SQRT3 * INV32, None, ALU.mult)
        for a, b, f in EDGE_FACTORS:
            dve.tensor_scalar(edge_w[:, a:b], edge_w[:, a:b], f, None, ALU.mult)
        for raw in (sv_raw, vs_raw):
            dve.tensor_scalar(raw[:, :], raw[:, :], INV_SQRT2048, None, ALU.mult).then_inc(scaled, 1)
        for n, (raw, w) in enumerate(splits):
            dve.wait_ge(high, n + 1)
            dve.tensor_tensor(w[:, 1, :], raw[:, :], w[:, 0, :].bitcast(F32), ALU.subtract)

    @block.scalar
    def _(act):
        act.wait_ge(loaded, 16 * len(loads))
        act.wait_ge(cleared, 1)
        big = agg[0:wide * 4 * T, :].rearrange("(t p j) f -> t p (j f)", p=R, j=4 * SUB)
        with act.Fori(0, wide) as t:
            act.dma_start(big[t], zeros[:, :]).then_inc(table_zero, 16)
        if rest:
            act.dma_start(agg[wide * 4 * T:rows, :].rearrange("(p j) f -> p (j f)", p=R),
                          zeros[:, 0:rest // R * D]).then_inc(table_zero, 16)
        act.activation(rot[:, :, :], rot_raw[:, :, :], ACT.Copy)
        act.activation(ident_r[:, :], ident[:, :], ACT.Copy)
        for n, (raw, w) in enumerate(splits):
            act.wait_ge(scaled, n + 1)
            act.activation(w[:, 0, :], raw[:, :], ACT.Copy).then_inc(high, 1)

    return wide + (1 if rest else 0)


EDGE_FACTORS = [(0, 64, INV8), (64, 128, INV_SQRT32), (128, 192, INV8), (192, 256, INV_SQRT32),
                (256, 384, INV_SQRT3 * INV_SQRT32), (384, 416, INV8),
                (416, 480, INV_SQRT32), (480, 544, INV_SQRT3 * INV_SQRT32)]
VV_AT = (0, 64, 160)
SV_AT = 128


def edges(nc, ctx, N, ET, x, src_col, src_row, dst_col, attr_t, consts, agg, ident, edge_w,
          table_zero, clears):
    def sb(name, shape, dt=F32):
        return ctx.enter_context(nc.sbuf_tensor(name, shape, dt))

    def sem(name):
        return ctx.enter_context(nc.semaphore(name))

    dst_i = [sb(f"dst_i{u}", [R, SUB], I32) for u in range(2)]
    src_i = [sb(f"src_i{u}", [R, SUB], I32) for u in range(2)]
    row_i = [sb(f"row_i{u}", [R, T], I32) for u in range(2)]
    at = [sb(f"at{u}", [R, SUB, 4]) for u in range(2)]
    xg = [sb(f"xg{u}", [R, SUB, D]) for u in range(2)]
    hg = [sb(f"hg{u}", [R, SUB, D]) for u in range(2)]
    stats = sb("stats", [R, SUB, 6])
    mean_var = sb("mean_var", [R, SUB, 2])
    std = sb("std", [R, SUB])
    var_eps = sb("var_eps", [R, SUB])
    rstd = [sb(f"rstd{u}", [R, SUB]) for u in range(2)]
    shift = [sb(f"shift{u}", [R, SUB]) for u in range(2)]
    turned = [sb(f"turned{u}", [128, 2, T]) for u in range(2)]
    msg = [sb(f"msg{u}", [R, SUB, D + SUB]) for u in range(2)]
    row_f = [sb(f"row_f{u}", [R, T]) for u in range(2)]
    col_f = [sb(f"col_f{u}", [R, SUB]) for u in range(2)]
    same = [sb(f"same{u}", [R, SUB, T]) for u in range(2)]
    before = sb("before", [R, R])
    seen = sb("seen", [R, SUB, R])
    own = [sb(f"own{u}", [R, SUB]) for u in range(2)]
    rank = sb("rank", [R, SUB])
    spare = sb("spare", [R, SUB])
    to_spare = [sb(f"to_spare{u}", [R, SUB]) for u in range(2)]
    to_f = sb("to_f", [R, SUB])
    to_i = [sb(f"to_i{u}", [R, SUB], I32) for u in range(2)]
    total = [sb(f"total{u}", [R, SUB, D + SUB]) for u in range(2)]

    tr = ctx.enter_context(nc.psum_tensor("tr", [128, 2, 512], F32))
    lin = [ctx.enter_context(nc.psum_tensor(f"lin{u}", [128, 512], F32)) for u in range(2)]
    prod = [ctx.enter_context(nc.psum_tensor(f"prod{u}", [128, 512], F32)) for u in range(2)]
    acc = ctx.enter_context(nc.psum_tensor("acc", [128, SUB, 256], F32))

    consts_in = sem("edge_consts_in")
    dst_in = [sem(f"dst_in{u}") for u in range(2)]
    src_in = [sem(f"src_in{u}") for u in range(2)]
    gathered = [sem(f"gathered{u}") for u in range(2)]
    var_ready = sem("var_ready")
    std_ready = sem("std_ready")
    scale_ready = sem("scale_ready")
    h_ready = sem("h_ready")
    turned_psum = sem("turned_psum")
    turned_ready = sem("turned_ready")
    prod_ready = sem("prod_ready")
    lin_ready = sem("lin_ready")
    msg_ready = sem("msg_ready")
    prod_used = sem("prod_used")
    keys_ready = sem("keys_ready")
    same_ready = sem("same_ready")
    summed = sem("summed")
    total_ready = sem("total_ready")
    index_ready = sem("index_ready")
    added = sem("added")
    scale_step = sem("edge_scale_step")
    msg_step = sem("edge_msg_step")
    key_step = sem("edge_key_step")
    index_step = sem("edge_index_step")
    passed = sem("edge_waits_passed")
    passed_dve = sem("edge_vector_waits_passed")
    passed_sp = sem("edge_loads_waits_passed")
    block = ctx.enter_context(nc.Block("edges"))

    def is0(n):
        return isinstance(n, int) and n == 0

    def under2(n):
        return isinstance(n, int) and n < 2

    def rounds(eng, body):
        for n in range(6):
            body(n, n % 2)
        with eng.Fori(3, ET // 2) as i:
            for u in range(2):
                body(i * 2 + u, u)
        for n in range(ET, ET + 3):
            body(n, n % 2)

    def runs(n):
        return not isinstance(n, int) or 0 <= n < ET

    @block.sync
    def _(sp):
        sp.dma_start(before[:, :], consts["before"]).then_inc(consts_in, 16)
        sp.dma_start(spare[:, :], consts["spare"]).then_inc(consts_in, 16)

        def load_dst(n, u):
            if not under2(n):
                sp.wait_ge(gathered[u], (n - u) * 32)
            sp.dma_start(dst_i[u][:, :], dst_col[n]).then_inc(dst_in[u], 16)

        def load(n, u):
            if not under2(n):
                sp.wait_ge(keys_ready, n - 1)
                sp.sem_inc(passed_sp, 1)
                sp.wait_ge(msg_ready, (n - 1) * SUB)
            sp.dma_start(src_i[u][:, :], src_col[n]).then_inc(src_in[u], 16)
            sp.dma_start(row_i[u][:, :], src_row[n].broadcast_to((R, T))).then_inc(src_in[u], 16)
            sp.dma_start(at[u][:, :, :], attr_t[n]).then_inc(src_in[u], 16)

        load_dst(0, 0)

        def body(n, u):
            if not (isinstance(n, int) and n + 1 >= ET):
                load_dst(n + 1, 1 - u)
            if runs(n):
                load(n, u)

        for n in range(6):
            body(n, n % 2)
        with sp.Fori(3, ET // 2 - 1) as i:
            for u in range(2):
                body(i * 2 + u, u)
        for n in range(ET - 2, ET):
            body(n, n % 2)

    @block.gpsimd
    def _(pool):
        def started():
            pool.sem_inc(passed, 1)

        def gather(n, u):
            pool.wait_ge(dst_in[u], (n - u) * 8 + 16)
            if not under2(n):
                pool.wait_ge(h_ready, n - 1)
            started()
            for a in range(SUB):
                pool.indirect_dma_start(xg[u][:, a, :], None, x,
                                        bass.IndirectOffsetOnAxis(ap=dst_i[u][:, a:a + 1], axis=0))\
                    .then_inc(gathered[u], 16)

        def scatter(n, u):
            pool.wait_ge(total_ready, n + 1)
            pool.wait_ge(index_ready, n + 1)
            if is0(n):
                pool.wait_ge(table_zero, 16 * clears)
            if not is0(n):
                pool.wait_ge(added, n * 16 * SUB)
            started()
            for a in range(SUB):
                pool.indirect_dma_start(agg, bass.IndirectOffsetOnAxis(ap=to_i[u][:, a:a + 1], axis=0),
                                        total[u][:, a, 0:D], None, compute_op=ALU.add)\
                    .then_inc(added, 16)

        gather(0, 0)

        def body(n, u):
            if not (isinstance(n, int) and n + 1 >= ET):
                gather(n + 1, 1 - u)
            if not (isinstance(n, int) and n < 3):
                scatter(n - 3, 1 - u)

        for n in range(6):
            body(n, n % 2)
        with pool.Fori(3, ET // 2 - 1) as i:
            for u in range(2):
                body(i * 2 + u, u)
        for n in range(ET - 2, ET + 3):
            body(n, n % 2)
        pool.wait_ge(added, ET * 16 * SUB)

    @block.vector
    def _(dve):
        for u in range(2):
            for b in range(SUB):
                nc.vector.memset(msg[u][:, b, D:D + b + 1], 0.0)
                if b < SUB - 1:
                    nc.vector.memset(msg[u][:, b, D + b + 1:D + SUB], 1.0)
        dve.wait_ge(consts_in, 32)

        def scales(n, u):
            dve.wait_ge(gathered[u], (n - u) * 32 + 16 * SUB)
            for a in range(SUB):
                nc.vector.bn_stats(stats[:, a, :], xg[u][:, a, :]).then_inc(scale_step, 1)
            dve.wait_ge(scale_step, n * 9 + 4)
            dve.sem_inc(passed_dve, 1)
            for a in range(SUB):
                nc.vector.bn_aggr(mean_var[:, a, :], stats[:, a, :]).then_inc(scale_step, 1)
            dve.wait_ge(scale_step, n * 9 + 8)
            nc.vector.tensor_scalar(var_eps[:, :], mean_var[:, :, 1], EPS, None, ALU.add).then_inc(var_ready, 1)

        def scales_end(n, u):
            dve.wait_ge(std_ready, n + 1)
            if not under2(n):
                dve.wait_ge(h_ready, n - 1)
            nc.vector.reciprocal(rstd[u][:, :], std[:, :]).then_inc(scale_step, 1)
            dve.wait_ge(scale_step, n * 9 + 9)
            nc.vector.scalar_tensor_tensor(out=shift[u][:, :], in0=mean_var[:, :, 0], scalar=-1.0,
                                           in1=rstd[u][:, :], op0=ALU.mult, op1=ALU.mult).then_inc(scale_ready, 1)

        def keys(n, u):
            dve.wait_ge(keys_ready, n + 1)
            if not under2(n):
                dve.wait_ge(summed, n - 1)
            for b in range(SUB):
                ins = nc.vector.tensor_scalar(same[u][:, b, :], row_f[u][:, :], col_f[u][:, b:b + 1], None,
                                              ALU.is_equal)
            ins.then_inc(same_ready, 1)

        def count(n, u):
            for b in range(SUB):
                nc.vector.scalar_tensor_tensor(out=seen[:, b, :], in0=row_f[u][:, b:T:SUB],
                                               scalar=col_f[u][:, b:b + 1], in1=before[:, :],
                                               op0=ALU.is_equal, op1=ALU.mult,
                                               accum_out=own[u][:, b:b + 1]).then_inc(key_step, 1)
            nc.vector.tensor_tensor(to_spare[u][:, :], spare[:, :], col_f[u][:, :], ALU.subtract)\
                .then_inc(key_step, 1)

        def index(n, u):
            dve.wait_ge(total_ready, n + 1)
            dve.wait_ge(key_step, n * 5 + 5)
            flat = total[u][:, :, :].rearrange("p a f -> p (a f)")
            counts = flat[:, D:D + (D + SUB + 1) * (SUB - 1) + 1:D + SUB + 1]
            nc.vector.tensor_tensor(rank[:, :], own[u][:, :], counts,
                                    ALU.add).then_inc(index_step, 1)
            dve.wait_ge(index_step, n * 2 + 1)
            nc.vector.scalar_tensor_tensor(out=to_f[:, :], in0=rank[:, :], scalar=1.0, in1=to_spare[u][:, :],
                                           op0=ALU.min, op1=ALU.mult).then_inc(index_step, 1)
            dve.wait_ge(index_step, n * 2 + 2)
            if not under2(n):
                dve.wait_ge(added, (n - 1) * 16 * SUB)
            nc.vector.tensor_tensor(to_i[u][:, :], to_f[:, :], col_f[u][:, :], ALU.add).then_inc(index_ready, 1)

        def messages(n, u, pair):
            if pair == 0:
                dve.wait_ge(src_in[u], (n - u) * 24 + 48)
            base = n * 12 + pair * 6
            groups = (2 * pair, 2 * pair + 1)
            done = 0

            def vv(a, c):
                m = msg[u][:, a, 0:S]
                return nc.vector.scalar_tensor_tensor(
                    out=m, in0=prod[a % 2][0:R, VV_AT[c]:VV_AT[c] + S], scalar=at[u][:, a, c:c + 1], in1=m,
                    op0=ALU.mult, op1=ALU.add)

            for a in groups:
                m = msg[u][:, a, 0:D]
                dve.wait_ge(lin_ready, n * SUB + a + 1)
                nc.vector.scalar_tensor_tensor(out=m, in0=lin[a % 2][0:R, D:2 * D], scalar=at[u][:, a, 3:4], in1=m,
                                               op0=ALU.mult, op1=ALU.add).then_inc(msg_step, 1)
            for a in groups:
                done += 1
                dve.wait_ge(msg_step, base + done)
                vv(a, 0).then_inc(msg_step, 1)
            for a in groups:
                for c in range(C3):
                    m = msg[u][:, a, S + V * c:S + V * c + V]
                    nc.vector.scalar_tensor_tensor(out=m, in0=prod[a % 2][0:R, SV_AT:SV_AT + V],
                                                   scalar=at[u][:, a, c:c + 1], in1=m, op0=ALU.mult, op1=ALU.add)
            for a in groups:
                done += 1
                dve.wait_ge(msg_step, base + done)
                vv(a, 1).then_inc(msg_step, 1)
            for a in groups:
                done += 1
                dve.wait_ge(msg_step, base + done)
                vv(a, 2).then_inc(msg_ready, 1)

        def body(n, u):
            if runs(n - 2):
                messages(n - 2, u, 0)
            if runs(n):
                scales(n, u)
            if runs(n - 2):
                count(n - 2, u)
                messages(n - 2, u, 1)
            if runs(n - 3):
                index(n - 3, 1 - u)
            if runs(n):
                scales_end(n, u)
            if runs(n - 1):
                keys(n - 1, 1 - u)

        rounds(dve, body)

    @block.scalar
    def _(act):
        def root(n, u):
            act.wait_ge(var_ready, n + 1)
            if not is0(n):
                act.wait_ge(scale_ready, n)
            nc.scalar.activation(std[:, :], var_eps[:, :], ACT.Sqrt).then_inc(std_ready, 1)

        def relu(n, u):
            act.wait_ge(scale_ready, n + 1)
            if not under2(n):
                act.wait_ge(turned_psum, n - 1)
            for a in range(SUB):
                sc, sh = rstd[u][:, a:a + 1], shift[u][:, a:a + 1]
                nc.scalar.activation(hg[u][:, a, 0:S], xg[u][:, a, 0:S], ACT.Relu, bias=sh, scale=sc)
                ins = nc.scalar.activation(hg[u][:, a, S:D].rearrange("p (c v) -> p c v", c=C3),
                                           xg[u][:, a, S:D].rearrange("p (v c) -> p c v", c=C3),
                                           ACT.Relu, bias=sh, scale=sc)
            ins.then_inc(h_ready, 1)

        def turned_out(n, u):
            act.wait_ge(turned_psum, n + 1)
            if not under2(n):
                act.wait_ge(prod_ready, (n - 1) * SUB)
            nc.scalar.activation(turned[u][:, :, :], tr[:, :, 0:T], ACT.Copy).then_inc(turned_ready, 1)

        def linear(n, u, pair):
            if pair == 0 and not under2(n):
                act.wait_ge(summed, n - 1)
            for a in (2 * pair, 2 * pair + 1):
                act.wait_ge(prod_ready, n * SUB + a + 1)
                nc.scalar.activation(msg[u][:, a, 0:D], lin[a % 2][0:R, 0:D], ACT.Copy).then_inc(lin_ready, 1)

        def sum_out(n, u):
            act.wait_ge(summed, n + 1)
            if not under2(n):
                act.wait_ge(added, (n - 1) * 16 * SUB)
            nc.scalar.activation(total[u][:, :, :], acc[0:R, :, 0:D + SUB], ACT.Copy).then_inc(total_ready, 1)

        def to_float(n, u):
            act.wait_ge(src_in[u], (n - u) * 24 + 48)
            if not under2(n):
                act.wait_ge(same_ready, n - 1)
                act.wait_ge(key_step, (n - 1) * 5)
            nc.scalar.activation(row_f[u][:, :], row_i[u][:, :], ACT.Copy)
            if not under2(n):
                act.wait_ge(index_ready, n - 1)
            nc.scalar.activation(col_f[u][:, :], src_i[u][:, :], ACT.Copy).then_inc(keys_ready, 1)

        def body(n, u):
            if runs(n - 2):
                linear(n - 2, u, 1)
            if runs(n):
                root(n, u)
            if runs(n - 3):
                sum_out(n - 3, 1 - u)
            if runs(n - 1):
                to_float(n - 1, 1 - u)
                linear(n - 1, 1 - u, 0)
            if runs(n):
                relu(n, u)
                turned_out(n, u)

        rounds(act, body)

    @block.tensor
    def _(pe):
        def turn(n, u):
            pe.wait_ge(h_ready, n + 1)
            if not is0(n):
                pe.wait_ge(turned_ready, n)
            for q, c in enumerate((0, V)):
                for a in range(SUB):
                    ins = nc.tensor.transpose(tr[:, q, R * a:R * a + R], hg[u][:, a, c:c + 128], ident[0:R, 0:R])
            ins.then_inc(turned_psum, 1)

        def products(n, u, pair):
            if pair == 0:
                pe.wait_ge(turned_ready, n + 1)
            for a in (2 * pair, 2 * pair + 1):
                q = a % 2
                if not (is0(n) and a < 2):
                    pe.wait_ge(msg_ready, n * SUB + a - 1)
                t1 = turned[u][:, 0, R * a:R * a + R]
                t2 = turned[u][:, 1, R * a:R * a + R]
                l2 = lin[q][0:R, 0:2 * D].rearrange("p (g f) -> p g f", g=2)
                nc.tensor.matmul(l2[:, :, 0:128], t1, edge_w[:, 0:256], start=True, stop=True)
                nc.tensor.matmul(prod[q][0:R, 0:160], t1, edge_w[:, 256:416], start=True, stop=True)
                nc.tensor.matmul(l2[:, :, 128:D], t2, edge_w[:, 416:480], start=True, stop=True)
                nc.tensor.matmul(prod[q][0:R, 160:224], t2, edge_w[:, 480:544], start=True, stop=True)\
                    .then_inc(prod_ready, 1)

        def sums(n, u, half):
            if half == 0:
                pe.wait_ge(msg_ready, n * SUB + SUB)
                pe.wait_ge(same_ready, n + 1)
                if not is0(n):
                    pe.wait_ge(total_ready, n)
            for a in (2 * half, 2 * half + 1):
                for b in range(SUB):
                    ins = nc.tensor.matmul(acc[0:R, a, 0:D + SUB], same[u][:, b, a:T:SUB], msg[u][:, b, :],
                                           start=(b == 0), stop=(b == SUB - 1))
            if half == 1:
                ins.then_inc(summed, 1)

        def body(n, u):
            if runs(n - 2):
                products(n - 2, u, 1)
            if runs(n - 3):
                sums(n - 3, 1 - u, 1)
            if runs(n - 1):
                products(n - 1, 1 - u, 0)
            if runs(n - 2):
                sums(n - 2, u, 0)
            if runs(n):
                turn(n, u)

        rounds(pe, body)


def nodes(nc, ctx, NT, x_t, agg_t, out_t, ident_r, w_ss, w_vv, w_sv, w_vs,
          rot_s_a, rot_s_b, rot_v_a, rot_v_b, sum_w, lin_s, lin_v, back_s, back_v):
    def sb(name, shape, dt=F32):
        return ctx.enter_context(nc.sbuf_tensor(name, shape, dt))

    def sem(name):
        return ctx.enter_context(nc.semaphore(name))

    X = [sb(f"X{u}", [R, SUB, D]) for u in range(2)]
    A = sb("A", [R, SUB, D])
    H = sb("H", [R, SUB, D])
    hl = sb("hl", [R, SUB, HL], F32R)
    O = sb("O", [R, SUB, D])
    stats = sb("nstats", [R, SUB, 6])
    mean_var = sb("nmean_var", [R, SUB, 2])
    std = sb("nstd", [R, SUB])
    var_eps = sb("nvar_eps", [R, SUB])
    rstd = sb("nrstd", [R, SUB])
    shift = sb("nshift", [R, SUB])
    parts = [[sb(f"parts{u}_{q}", [128, 3, T], F32R) for q in range(2)] for u in range(2)]
    s_a = sb("s_a", [128, JS, T])
    s_b = sb("s_b", [128, KS - KS_G, T])
    v_a = [sb(f"v_a{u}", [128, C3, JV, T]) for u in range(2)]
    v_b = [sb(f"v_b{u}", [128, C3, T]) for u in range(2)]
    NP = 3
    P = [sb(f"P{r}", [128, max(SS_SIZES), T]) for r in range(NP)]
    VP = [sb(f"VP{r}", [128, C3, JV, T]) for r in range(2)]
    G = [sb(f"G{r}", [128, JG, T]) for r in range(2)]
    u0 = sb("u0", [128, T])
    u1 = sb("u1", [128, T])

    U0 = ctx.enter_context(nc.psum_tensor("U0", [128, 512], F32))
    U1 = ctx.enter_context(nc.psum_tensor("U1", [128, 512], F32))
    NR = 4
    ring = [ctx.enter_context(nc.psum_tensor(f"ring{r}", [128, 512], F32)) for r in range(NR)]
    prep = ctx.enter_context(nc.psum_tensor("prep", [128, 2, 512], F32))

    x_in = [sem(f"x_in{u}") for u in range(2)]
    a_in = sem("a_in")
    pad_ready = sem("pad_ready")
    var_ready = sem("nvar_ready")
    std_ready = sem("nstd_ready")
    scale_ready = sem("nscale_ready")
    h_ready = sem("nh_ready")
    hi_ready = sem("hi_ready")
    hl_ready = sem("hl_ready")
    prep_ready = sem("prep_ready")
    prep_used = sem("prep_used")
    source_ready = sem("source_ready")
    made = sem("made")
    made_g = sem("made_g")
    half_added = sem("half_added")
    added_v = sem("added_v")
    taken = sem("taken")
    taken_g = sem("taken_g")
    taken_v = sem("taken_v")
    u0_out = sem("u0_out")
    u1_out = sem("u1_out")
    back_ready = sem("back_ready")
    out_made = sem("out_made")
    stored = sem("stored")
    step = sem("node_vector_step")
    passed_dve = sem("node_vector_waits_passed")
    block = ctx.enter_context(nc.Block("nodes"))

    def vv(k):
        return [("vv", k, c) for c in range(C3)]

    def sv(k):
        return [("sv", k, 0), ("vs", k, 0)]

    ORDER = "vsqsvqsqsvssqvss"
    ss = [("ss", sum(SS_SIZES[:i]) // JS, sum(SS_SIZES[:i]) % JS) for i in range(len(SS_SIZES))]
    ss_size = {ch: size for ch, size in zip(ss, SS_SIZES)}
    chunks = []
    for i, what in enumerate(ORDER):
        n = ORDER[:i].count(what)
        chunks += vv(n) if what == "v" else sv(n) if what == "s" else [ss[n]]
    NCH = len(chunks)
    assert NCH % NR == 0
    p_before = [sum(ch[0] != "vv" for ch in chunks[:n]) for n in range(NCH + 1)]
    NPC = p_before[NCH]
    vv_at = [max(n for n, ch in enumerate(chunks) if ch[:2] == ("vv", k)) for k in range(KV)]
    last_ss = max(n for n, ch in enumerate(chunks) if ch[0] == "ss")
    first_j = SS_DVE % JS
    order_j = [(first_j + i) % JS for i in range(JS)]
    chunks_g = [(i // JS, order_j[(i - first_j) % JS]) for i in range(SS_DVE, JS * KS, JG)]
    NG = len(chunks_g)
    order_g = ["g", "s0", "g", "g", "v", "g", "g", "s1", "v", "g", "g", "g", "v", "g", "g", "v"]
    G_AFTER = [0, 3, 10, 10, 15, 16, 19, 21, 25, 29]
    V_AFTER = [7, 14, 22, 30]
    RIDERS = ["v0", "v1", "v2"]
    after = {n: [("g", m) for m in range(NG) if G_AFTER[m] == n and f"g{m}" not in RIDERS]
             + [("v", m) for m in range(KV) if V_AFTER[m] == n and f"v{m}" not in RIDERS] for n in range(NCH)}
    rides = {}
    for start, name in sorted(((V_AFTER if name[0] == "v" else G_AFTER)[int(name[1:])], name) for name in RIDERS):
        free = [n for n in range(start, NCH) if chunks[n][0] in ("sv", "vs") and n not in rides][:4]
        assert len(free) == 4
        for i, n in enumerate(free):
            rides[n] = (name[0], int(name[1:]), i)
    for what in "gv":
        done = sorted([(n, m) for n in after for w, m in after[n] if w == what]
                      + [(n - 0.5, rides[n][1]) for n in rides if rides[n][0] == what and rides[n][2] == 3])
        assert [m for _, m in done] == list(range(NG if what == "g" else KV))
    prep_steps = [("turn", 1, g) for g in range(3)]
    prep_steps += [("v_b", c, 0) for c in range(C3)]
    prep_steps += [("turn", 0, g) for g in range(3)]
    prep_steps += [("v_a", c, j) for c in range(C3) for j in range(JV)]
    prep_steps += [("s_b", k, 0) for k in range(KS_G, KS - 1)]
    prep_steps += [("s_a", j, 0) for j in order_j]
    prep_steps += [("s_b", KS - 1, 0)]
    NPREP = len(prep_steps)
    prep_after = [3, 3, 4, 5, 6, 6, 12, 15, 15, 16, 17, 18, 19, 19, 20, 20, 21, 21, 24, 24, 25, 27, 27, 28, 29, 29]
    STEP = 2
    TURNED_SUMS, TURNED_H = 3, 9
    FIRST_S = prep_steps.index(("s_b", KS_G, 0))
    FIRST_SA = prep_steps.index(("s_a", order_j[0], 0))
    operands_g = [max([prep_steps.index(("s_b", k, 0))]
                      + [prep_steps.index(("s_a", j, 0)) for j in range(j0, j0 + JG)]) for k, j0 in chunks_g]

    def last_g(what, n):
        return max(m for m, (k, j0) in enumerate(chunks_g) if (k == n if what == "s_b" else j0 <= n < j0 + JG))

    BACK, FINISH, SCALES, SCALES_END = 0, 4, 6, 8
    ROOT = 3
    NORMALISE = 4

    def tiles(eng, body):
        for t in range(2):
            body(t, t, False)
        with eng.Fori(1, NT // 2 - 1) as i:
            for u in range(2):
                body(i * 2 + u, u, False)
        for t in range(NT - 2, NT):
            body(t, t % 2, t == NT - 1)

    def is0(t):
        return isinstance(t, int) and t == 0

    @block.sync
    def _(sp):
        def load(t, u):
            if not is0(t):
                sp.wait_ge(hl_ready, t * 2 - 1)
            sp.dma_start(A[:, :, :], agg_t[t]).then_inc(a_in, 16)
            if not (isinstance(t, int) and t < 2):
                sp.wait_ge(out_made, t - 1)
            sp.dma_start(X[u][:, :, :], x_t[t]).then_inc(x_in[u], 16)

        def store(t):
            sp.wait_ge(out_made, t + 1)
            sp.dma_start(out_t[t], O[:, :, :]).then_inc(stored, 16)

        load(0, 0)
        load(1, 1)

        def body(t, u, last):
            if not is0(t):
                if not last:
                    load(t + 1, 1 - u)
                store(t - 1)

        tiles(sp, body)
        store(NT - 1)
        sp.wait_ge(stored, 16 * NT)

    @block.gpsimd
    def _(pool):
        pool.memset(hl[:, :, HL - 64:HL].bitcast(F32), 0.0).then_inc(pad_ready, 1)

        def split(t, q):
            frm = (A, H)[q]
            pool.wait_ge(hi_ready, t * 2 + q + 1)
            v = hl[:, :, 2 * S:2 * S + 2 * C3 * V].rearrange("p j (c g v) -> p j c g v", c=C3, g=2)
            nc.gpsimd.tensor_tensor(hl[:, :, S:2 * S], frm[:, :, 0:S], hl[:, :, 0:S].bitcast(F32), ALU.subtract)
            nc.gpsimd.tensor_tensor(v[:, :, :, 1, :],
                                    frm[:, :, S:D].rearrange("p j (c v) -> p j c v", c=C3),
                                    v[:, :, :, 0, :].bitcast(F32),
                                    ALU.subtract).then_inc(hl_ready, 1)

        def products(t, g):
            k, j0 = chunks_g[g]
            pool.wait_ge(prep_used, t * NPREP + operands_g[g] + 1)
            if not (is0(t) and g < 2):
                pool.wait_ge(taken_g, t * NG + g - 1)
            nc.gpsimd.tensor_tensor(
                G[g % 2][:, :, :], s_a[:, j0:j0 + JG, :],
                s_b[:, k - KS_G, :].unsqueeze(1).broadcast_to((128, JG, T)), ALU.mult).then_inc(made_g, 1)

        def add_components(t, k):
            vp = VP[k % 2]
            pool.wait_ge(made, t * NCH + vv_at[k] + 1)
            nc.gpsimd.tensor_tensor(vp[:, 0, :, :], vp[:, 0, :, :], vp[:, 1, :, :], ALU.add)\
                .then_inc(half_added, 1)
            pool.wait_ge(half_added, t * KV + k + 1)
            nc.gpsimd.tensor_tensor(vp[:, 0, :, :], vp[:, 0, :, :], vp[:, 2, :, :], ALU.add)\
                .then_inc(added_v, 1)

        split(0, 0)
        split(0, 1)

        def body(t, u, last):
            for i, what in enumerate(order_g):
                n = order_g[:i].count(what)
                if what == "g":
                    products(t, n)
                elif what == "v":
                    add_components(t, n)
                elif not last:
                    split(t + 1, 0 if what == "s0" else 1)

        tiles(pool, body)

    @block.scalar
    def _(act):
        def high(t, q):
            frm = (A, H)[q]
            v = hl[:, :, 2 * S:2 * S + 2 * C3 * V].rearrange("p j (c g v) -> p j c g v", c=C3, g=2)
            nc.scalar.activation(hl[:, :, 0:S], frm[:, :, 0:S], ACT.Copy)
            nc.scalar.activation(v[:, :, :, 0, :],
                                 frm[:, :, S:D].rearrange("p j (c v) -> p j c v", c=C3),
                                 ACT.Copy).then_inc(hi_ready, 1)

        def high_sums(t):
            act.wait_ge(a_in, t * 16 + 16)
            if not is0(t):
                act.wait_ge(prep_ready, (t - 1) * NPREP + TURNED_H)
            high(t, 0)

        def root(t):
            act.wait_ge(var_ready, t + 1)
            if not is0(t):
                act.wait_ge(scale_ready, t)
            nc.scalar.activation(std[:, :], var_eps[:, :], ACT.Sqrt).then_inc(std_ready, 1)

        def normalise(t, u):
            act.wait_ge(scale_ready, t + 1)
            if not is0(t):
                act.wait_ge(hl_ready, t * 2)
            for a in range(SUB):
                sc, sh = rstd[:, a:a + 1], shift[:, a:a + 1]
                nc.scalar.activation(H[:, a, 0:S], X[u][:, a, 0:S], ACT.Relu, bias=sh, scale=sc)
                ins = nc.scalar.activation(H[:, a, S:D].rearrange("p (c v) -> p c v", c=C3),
                                           X[u][:, a, S:D].rearrange("p (v c) -> p c v", c=C3),
                                           ACT.Relu, bias=sh, scale=sc)
            ins.then_inc(h_ready, 1)
            act.wait_ge(h_ready, t + 1)
            act.wait_ge(prep_ready, t * NPREP + TURNED_SUMS)
            high(t, 1)

        def take(t, u, n):
            what, a, b = prep_steps[n]
            if what in ("s_a", "s_b") and not is0(t):
                act.wait_ge(made_g, (t - 1) * NG + last_g(what, a) + 1)
            if n == FIRST_SA and not is0(t):
                act.wait_ge(made, (t - 1) * NCH + last_ss + 1)
            act.wait_ge(prep_ready, t * NPREP + n + 1)
            to = {"turn": lambda: parts[u][a][:, b, :], "s_a": lambda: s_a[:, a, :],
                  "s_b": lambda: s_b[:, a - KS_G, :], "v_a": lambda: v_a[u][:, a, b, :],
                  "v_b": lambda: v_b[u][:, a, :]}[what]()
            frm = prep[:, n % 2, 0:T]
            if what == "turn":
                to = to.rearrange("p (i r) -> p i r", i=SUB)
                frm = prep[:, n % 2, 0:SUB * RE].rearrange("p (i r) -> p i r", i=SUB)[:, :, 0:R]
            nc.scalar.activation(to, frm, ACT.Copy).then_inc(prep_used, 1)

        def prepare(t, u):
            high_sums(t)
            for n in range(NPREP):
                if n == ROOT:
                    root(t)
                if n == NORMALISE:
                    normalise(t, u)
                take(t, u, n)

        prepare(0, 0)

        def body(t, u, last):
            if not last:
                prepare(t + 1, 1 - u)
            act.wait_ge(taken, t * NPC + p_before[last_ss] + 1)
            act.wait_ge(taken_g, (t + 1) * NG)
            act.wait_ge(taken_v, (t + 1) * KV)
            if not is0(t):
                act.wait_ge(back_ready, t)
            nc.scalar.activation(u0[:, :], U0[:, 0:T], ACT.Copy).then_inc(u0_out, 1)
            act.wait_ge(taken, (t + 1) * NPC)
            nc.scalar.activation(u1[:, :], U1[:, 0:T], ACT.Copy).then_inc(u1_out, 1)

        tiles(act, body)

    @block.vector
    def _(dve):
        def scales(t, u):
            dve.wait_ge(x_in[u], (t - u) * 8 + 16)
            if not is0(t):
                dve.wait_ge(h_ready, t)
            for a in range(SUB):
                nc.vector.bn_stats(stats[:, a, :], X[u][:, a, :]).then_inc(step, 1)
            dve.wait_ge(step, t * 9 + 4)
            dve.sem_inc(passed_dve, 1)
            for a in range(SUB):
                nc.vector.bn_aggr(mean_var[:, a, :], stats[:, a, :]).then_inc(step, 1)
            dve.wait_ge(step, t * 9 + 8)
            nc.vector.tensor_scalar(var_eps[:, :], mean_var[:, :, 1], EPS, None, ALU.add).then_inc(var_ready, 1)

        def scales_end(t):
            dve.wait_ge(std_ready, t + 1)
            nc.vector.reciprocal(rstd[:, :], std[:, :]).then_inc(step, 1)
            dve.wait_ge(step, t * 9 + 9)
            nc.vector.scalar_tensor_tensor(out=shift[:, :], in0=mean_var[:, :, 0], scalar=-1.0,
                                           in1=rstd[:, :], op0=ALU.mult, op1=ALU.mult).then_inc(scale_ready, 1)

        def product(t, u, n):
            kind, k, c = chunks[n]
            dve.wait_ge(source_ready, t * NCH + n + 1)
            if n == 0:
                dve.wait_ge(prep_used, t * NPREP + FIRST_S)
            if kind == "ss":
                dve.wait_ge(prep_used, t * NPREP + FIRST_SA + JS)
            p = P[p_before[n] % NP]
            if kind == "vv":
                if c == 0 and not (is0(t) and k < 2):
                    dve.wait_ge(taken_v, t * KV + k - 1)
                out, b = VP[k % 2][:, c, :, :], v_a[u][:, c, :, :]
            else:
                before_it = reuse[n]
                if before_it is not None and not (is0(t) and before_it < 0):
                    dve.wait_ge(taken, t * NPC + before_it + 1)
                if kind == "ss":
                    size = ss_size[chunks[n]]
                    out, b = p[:, 0:size, :], s_a[:, c:c + size, :]
                elif kind == "sv":
                    out, b = p[:, 0:C3, :], v_b[u][:, :, :]
                else:
                    out, b = p[:, 0:C3, :], v_a[u][:, :, 0, :]
            nc.vector.tensor_tensor(out, ring[n % NR][:, 0:T].unsqueeze(1).broadcast_to((128, out.shape[1], T)), b,
                                    ALU.mult).then_inc(made, 1)

        reuse = []
        for n in range(NCH):
            m = p_before[n]
            same = [q for q in range(-NPC, m) if (q + NPC if q < 0 else q) % NP == m % NP]
            reuse.append(max(same))

        def finish(t, u):
            dve.wait_ge(back_ready, t + 1)
            if not is0(t):
                dve.wait_ge(stored, t * 16)
            nc.vector.tensor_tensor(O[:, :, :], X[u][:, :, :], prep[0:R, :, :].rearrange(
                "p b (h f) -> p (b h) f", h=2)[:, :, 0:D], ALU.add).then_inc(out_made, 1)

        scales(0, 0)
        scales_end(0)

        def body(t, u, last):
            for n in range(NCH):
                product(t, u, n)
                if n == FINISH and not is0(t):
                    finish(t - 1, 1 - u)
                if n == SCALES and not last:
                    scales(t + 1, 1 - u)
                if n == SCALES_END and not last:
                    scales_end(t + 1)

        tiles(dve, body)
        finish(NT - 1, (NT - 1) % 2)

    @block.tensor
    def _(pe):
        pe.wait_ge(pad_ready, 1)

        def rotate(to, u, q, c, sel):
            if c is None:
                return nc.tensor.matmul(to, sel, parts[u][q][:, 0, :], start=True, stop=True)
            return nc.tensor.matmul(to, sel[c % 2], parts[u][q][:, 1 + c // 2, :], start=True, stop=True)

        def prepare(t, u, n):
            what, a, b = prep_steps[n]
            to = prep[:, n % 2, 0:T]
            if n == 0 and not (isinstance(t, int) and t < 2):
                pe.wait_ge(out_made, t - 1)
            if what == "turn" and b == 0:
                pe.wait_ge(hl_ready, t * 2 + (1 if a else 2))
            if n >= 2:
                pe.wait_ge(prep_used, t * NPREP + n - 1)
            elif not is0(t):
                pe.wait_ge(prep_used, t * NPREP)
            if n in (TURNED_SUMS, TURNED_H):
                pe.wait_ge(prep_used, t * NPREP + n)
            if what == "turn":
                for i in range(SUB):
                    ins = nc.tensor.matmul(prep[:, n % 2, RE * i:RE * i + RE], hl[:, i, 128 * b:128 * b + 128],
                                           ident_r[0:R, 0:RE], start=True, stop=True)
            elif what == "s_a":
                ins = rotate(to, u, 0, None, rot_s_a[a])
            elif what == "s_b":
                ins = rotate(to, u, 1, None, rot_s_b[a])
            elif what == "v_a":
                ins = rotate(to, u, 0, a, [rot_v_a[q][b] for q in range(2)])
            else:
                ins = rotate(to, u, 1, a, [rot_v_b[q][0] for q in range(2)])
            ins.then_inc(prep_ready, 1)

        def source(t, u, n):
            kind, k, c = chunks[n]
            to = ring[n % NR][:, 0:T]
            if not (is0(t) and n < NR):
                pe.wait_ge(made, t * NCH + n - NR + 1)
            if kind == "ss":
                ins = rotate(to, u, 1, None, rot_s_b[k])
            elif kind == "vv":
                ins = rotate(to, u, 1, c, [rot_v_b[q][k] for q in range(2)])
            else:
                q, w = (0, w_sv) if kind == "sv" else (1, w_vs)
                for half in range(2):
                    ins = nc.tensor.matmul(to, w[:, half, 128 * k:128 * k + 128], parts[u][q][:, 0, :],
                                           start=(half == 0), stop=(half == 1))
            ins.then_inc(source_ready, 1)

        first_p = min(n for n in range(NCH) if chunks[n][0] != "vv")
        plan = [("lin_s", 0, 0)]
        for n in range(NCH):
            if n == first_p:
                plan.append(("lin_v", 0, 0))
            if chunks[n][0] != "vv":
                plan.append(chunks[n])
            for what, m in after.get(n, []):
                plan.append(("ss_g", *chunks_g[m]) if what == "g" else ("vv", m, 0))

        def groups(kind):
            return [0, 1] if kind in ("lin_s", "ss", "ss_g", "vv") else [2 + c for c in range(C3)]

        stops = {g: max(n for n, st in enumerate(plan) if g in groups(st[0])) for g in range(2 + C3)}

        def accumulate(at, u, p):
            kind, k, c = plan[at]
            start = kind in ("lin_s", "lin_v")

            def add(g, w, moving, end=True):
                to = U0[S * g:S * g + S, 0:T] if g < 2 else U1[V * (g - 2):V * (g - 2) + V, 0:T]
                return nc.tensor.matmul(to, w, moving, start=start, stop=(at == stops[g] and end))

            if kind == "lin_s":
                for half in range(2):
                    ins = nc.tensor.matmul(U0[:, 0:T], lin_s[:, half, :], parts[u][0][:, 0, :],
                                           start=(half == 0), stop=False)
            elif kind == "lin_v":
                for c in range(C3):
                    ins = add(2 + c, lin_v[:, :], v_a[u][:, c, 0, :])
            elif kind in ("ss", "ss_g", "vv"):
                size = {"ss": ss_size.get(plan[at]), "ss_g": JG, "vv": JV}[kind]
                for m in range(size):
                    w = w_vv[:, m * KV + k, :] if kind == "vv" else w_ss[:, (c + m) * KS + k, :]
                    ins = add(m % 2, w, p[:, m, :], m >= size - 2)
            else:
                for c in range(C3):
                    ins = add(2 + c, sum_w[:, k, :], p[:, c, :])
            return ins

        first_ride = min(rides)
        last_ride = max(n for n in rides if rides[n][2] == 2)

        def ride(n):
            what, m, piece = rides[n]
            j, half = piece // 2, piece % 2
            if what == "g":
                k, j0 = chunks_g[m]
                w, moving = w_ss[:, (j0 + j) * KS + k, :], G[m % 2][:, j, :]
            else:
                w, moving = w_vv[:, j * KV + m, :], VP[m % 2][:, 0, j, :]
            to = (U0 if half else U1)[C3 * V:C3 * V + V, 0:T]
            return nc.tensor.matmul(to, w[:, V * half:V * half + V], moving, start=(n == first_ride and not half),
                                    stop=(n == last_ride))

        def back(t):
            pe.wait_ge(u0_out, t + 1)
            pe.wait_ge(u1_out, t + 1)
            pe.wait_ge(prep_used, NT * NPREP if isinstance(t, int) and t == NT - 1 else (t + 2) * NPREP)
            for a in range(SUB):
                to = prep[0:R, a // 2, 256 * (a % 2):256 * (a % 2) + D]
                nc.tensor.matmul(to, u1[:, R * a:R * a + R], back_v[:, :], start=True, stop=False)
                ins = nc.tensor.matmul(to[:, 0:S], u0[:, R * a:R * a + R], back_s[:, :], start=False, stop=True)
            ins.then_inc(back_ready, 1)

        def body(t, u, last):
            pe.wait_ge(prep_used, t * NPREP + FIRST_S)
            if is0(t):
                for n in range(3):
                    source(t, u, n)
            if not is0(t):
                pe.wait_ge(u0_out, t)
            accumulate(0, u, None)
            at = 1
            prepared = 0
            for n in range(NCH):
                if n == first_p:
                    if not is0(t):
                        pe.wait_ge(u1_out, t)
                    accumulate(at, u, None)
                    at += 1
                if chunks[n][0] != "vv":
                    pe.wait_ge(made, t * NCH + n + 1)
                    ins = accumulate(at, u, P[p_before[n] % NP])
                    ins.then_inc(taken, 1)
                    at += 1
                if n in rides:
                    what, m, piece = rides[n]
                    if piece == 0 and what == "g":
                        pe.wait_ge(made_g, t * NG + m + 1)
                    if piece == 0 and what == "v":
                        pe.wait_ge(added_v, t * KV + m + 1)
                    ins = ride(n)
                    if piece == 3:
                        ins.then_inc(taken_g if what == "g" else taken_v, 1)
                for m in ahead[n]:
                    if m < NCH:
                        source(t, u, m)
                    elif not last:
                        source(t + 1, 1 - u, m - NCH)
                for what, m in after.get(n, []):
                    if what == "g":
                        pe.wait_ge(made_g, t * NG + m + 1)
                        ins = accumulate(at, u, G[m % 2]).then_inc(taken_g, 1)
                    else:
                        pe.wait_ge(added_v, t * KV + m + 1)
                        ins = accumulate(at, u, VP[m % 2][:, 0, :, :]).then_inc(taken_v, 1)
                    at += 1
                if n == BACK and not is0(t):
                    back(t - 1)
                while not last and prepared < NPREP and prep_after[prepared] <= n:
                    prepare(t + 1, 1 - u, prepared)
                    prepared += 1

        ahead = [[] for _ in range(NCH)]
        for n in range(0, NCH, STEP):
            ahead[n] = [m for m in range(n + 3, n + 3 + STEP) if m < NCH + 3]

        for n in range(NPREP):
            prepare(0, 0, n)
        tiles(pe, body)
        back(NT - 1)


def shape_constants():
    import numpy as np

    r, q = np.arange(128)[:, None], np.arange(128)[None, :]
    ident = (r == q).astype(np.float32)
    rot = []
    b, l = q // S, q % S
    rot += [r % S == (l + j) % S for j in range(JS)]
    rot += [r % S == (l + 8 * k + 32 * b) % S for k in range(KS)]
    b, l = q // V, q % V
    rot += [(r // 64 == g) & (r % V == (l + j) % V) for g in range(2) for j in range(JV)]
    rot += [(r // 64 == g) & (r % V == (l + 2 * b + 8 * k) % V) for g in range(2) for k in range(KV)]
    rot = np.stack(rot, axis=1).astype(np.float32)
    w = np.arange(V)[None, None, :]
    sum_w = (w == 4 * np.arange(KW)[None, :, None] + (np.arange(128) // V)[:, None, None]).astype(np.float32)
    lin_s_eye = ((r % S == q) & (q < S)).astype(np.float32)
    lin_v_eye = np.eye(128, V, dtype=np.float32)
    back_s = (np.arange(128)[:, None] % S == np.arange(S)[None, :]).astype(np.float32)
    cv = np.arange(C3 * V)
    back_v = np.zeros((128, D), np.float32)
    back_v[0:C3 * V, S:D] = C3 * (cv[:, None] % V) + cv[:, None] // V == cv[None, :]
    back_v[C3 * V:, 0:V] = np.eye(V)
    before = (np.arange(R)[None, :] < np.arange(R)[:, None]).astype(np.float32)
    return {"ident": ident, "rot": rot, "sum_w": sum_w, "lin_s_eye": lin_s_eye, "lin_v_eye": lin_v_eye,
            "back_s": back_s, "back_v": back_v, "before": before}


def weight_layouts(w):
    import numpy as np

    f = np.float32
    out = {}
    q = np.arange(128)
    b, l = q // S, q % S
    out["w_ss"] = np.stack([w["Wu_ss"][(l + j) % S, (l + 8 * k + 32 * b) % S] for j in range(JS) for k in range(KS)],
                           axis=1)
    b, l = q // V, q % V
    out["w_vv"] = np.stack([w["Wu_vv"][(l + j) % V, (l + 2 * b + 8 * k) % V] for j in range(JV) for k in range(KV)],
                           axis=1)
    rows = np.arange(128)[:, None] % S
    out["w_sv"] = np.concatenate([w["Wu_sv"][rows, ((l + 2 * b) % V)[None], (4 * k + b)[None]] for k in range(KW)],
                                 axis=1)
    out["w_vs"] = np.concatenate([w["Wu_vs"][l[None], rows, (4 * k + b)[None]] for k in range(KW)], axis=1)
    out["lin_s"] = np.zeros((128, 128), f)
    out["lin_s"][0:S, 0:S] = out["lin_s"][S:2 * S, 0:S] = w["Lu_s"]
    out["lin_v"] = np.zeros((128, V), f)
    out["lin_v"][0:V] = w["Lu_v"]
    e = np.zeros((128, 544), f)
    e[0:S, 0:64], e[0:S, 128:192], e[0:S, 384:416] = w["Lm_s"], w["Wm_ss"], w["Wm_sv"]
    for c in range(2):
        rows = slice(S + V * c, S + V * c + V)
        e[rows, 64 + V * c:64 + V * c + V] = w["Lm_v"]
        e[rows, 192 + V * c:192 + V * c + V] = w["Wm_vs"]
        e[rows, 256 + S * c:256 + S * c + S] = w["Wm_vv"]
    e[96:128, 416:448], e[96:128, 448:480], e[96:128, 480:544] = w["Lm_v"], w["Wm_vs"], w["Wm_vv"]
    out["edge_w"] = e
    return {n: np.ascontiguousarray(a) for n, a in out.items()}


def kernel(x, src, dst, edge_attr_4, node_vec1, **weights):
    import numpy as np
    import concourse.bacc as bacc
    from concourse.bass_utils import run_bass_kernel_spmd

    nc = bacc.Bacc("TRN2", target_bir_lowering=False, num_devices=1)
    arrays = {}

    def take(name, a):
        arrays[name] = a = np.ascontiguousarray(a)
        return nc.dram_tensor(name, a.shape, mybir.dt.from_np(a.dtype), kind="ExternalInput").ap()

    x_ap, src_ap, dst_ap, attr_ap = (take(n, a) for n, a in
                                     (("x", x), ("src", src), ("dst", dst), ("attr", edge_attr_4)))
    consts = shape_constants()
    consts["spare"] = (x.shape[0] + SUB * np.arange(R)[:, None] + np.arange(SUB)[None, :]).astype(np.float32)
    consts = {n: take("const_" + n, a) for n, a in consts.items()}
    layouts = weight_layouts({n.removeprefix("L0_gnn_"): np.asarray(a) for n, a in weights.items()})
    layouts = {n: take("weight_" + n, a) for n, a in layouts.items()}
    out = nc.dram_tensor("out", x.shape, F32, kind="ExternalOutput").ap()
    program(nc, x_ap, src_ap, dst_ap, attr_ap, consts, layouts, out)
    return run_bass_kernel_spmd(nc, [arrays], core_ids=[0]).results[0]["out"]
```
